# Optimizing a Trainium2 kernel written in Bass

```python
import numpy as np
import jax
import jax.numpy as jnp

def _softmax(x, axis=-1):
    return jax.nn.softmax(x, axis=axis)

def _gelu(x):
    return jax.nn.gelu(x, approximate=True)

def _silu(x):
    return jax.nn.silu(x)

def _sigmoid(x):
    return jax.nn.sigmoid(x)

def _layernorm(x, axis=-1, eps=1e-05):
    m = jnp.mean(x, axis=axis, keepdims=True)
    v = jnp.var(x, axis=axis, keepdims=True)
    return (x - m) / jnp.sqrt(v + eps)

def _scatter_add(tgt, idx, src, axis=0):
    return tgt.at[idx].add(src)

def _segment_sum(src, seg, n):
    return jax.ops.segment_sum(src, seg, n)
kernel_name = 'mk_prb_d1_jaxref_r8_c1e1c4'

def setup_inputs(seed: int=0):
    np.random.seed(seed)
    _w = jnp.asarray

    def _L0_attn_setup():
        import jax, jax.numpy as jnp
        import numpy as np
        D_MODEL = 128
        N_HEADS = 16
        HEAD_DIM = D_MODEL // N_HEADS
        D_LATENT = 32
        LAMBDA_DECAY = 0.01
        TIME_STEP = 0.01
        CLAMP = 10000.0

        def _reference_tuple_inner(x, Wq, Wk, Wv, Wo, W_down_kv, W_up_k, W_up_v):
            B, S, _ = x.shape
            q = x @ Wq
            k = x @ Wk
            v = x @ Wv
            latent_kv = (k + v) @ W_down_kv
            k_rec = latent_kv @ W_up_k
            v_rec = latent_kv @ W_up_v

            def heads(t):
                return t.reshape(B, S, N_HEADS, HEAD_DIM).transpose(0, 2, 1, 3)
            qh, kh, vh = (heads(q), heads(k_rec), heads(v_rec))
            scale = 1.0 / (jnp.sqrt(jnp.float32(D_MODEL)) + 1e-08)
            scores = jnp.einsum('bhqd,bhkd->bhqk', qh, kh) * scale
            scores = jnp.clip(jnp.nan_to_num(scores, nan=-1000000000.0), -CLAMP, CLAMP)
            idx = jnp.arange(S, dtype=jnp.float32)
            decay = jnp.exp(-LAMBDA_DECAY * TIME_STEP * jnp.abs(idx[:, None] - idx[None, :]))
            scores = scores * decay[None, None, :, :]
            scores = jnp.clip(jnp.nan_to_num(scores, nan=-1000000000.0), -CLAMP, CLAMP)
            attn = jax.nn.softmax(scores, axis=-1)
            out = jnp.einsum('bhqk,bhkd->bhqd', attn, vh)
            out = out.transpose(0, 2, 1, 3).reshape(B, S, D_MODEL)
            return (out @ Wo, latent_kv)
        key = jax.random.key(seed)
        ks = jax.random.split(key, 8)
        B, S = (2, 256)

        def w(k, i, o):
            return jax.random.normal(k, (i, o), dtype=jnp.float32) * 0.02
        return {'x': jax.random.normal(ks[0], (B, S, D_MODEL), dtype=jnp.float32), 'Wq': w(ks[1], D_MODEL, D_MODEL), 'Wk': w(ks[2], D_MODEL, D_MODEL), 'Wv': w(ks[3], D_MODEL, D_MODEL), 'Wo': w(ks[4], D_MODEL, D_MODEL), 'W_down_kv': w(ks[5], D_MODEL, D_LATENT), 'W_up_k': w(ks[6], D_LATENT, D_MODEL), 'W_up_v': w(ks[7], D_LATENT, D_MODEL)}
    _L0_attn_in = _L0_attn_setup()

    def _L0_ffn_setup():
        import jax, jax.numpy as jnp
        import numpy as np
        E = 8
        TOP_K = 2
        H = 128
        F = 512
        LN_EPS = 1e-12
        key = jax.random.key(seed)
        ks = jax.random.split(key, 9)
        s = lambda k, shape, scale: jax.random.normal(k, shape, dtype=jnp.float32) * scale
        return {'hidden_states': s(ks[0], (4, 256, H), 1.0), 'Wr': s(ks[1], (E, H), 0.02), 'br': jnp.zeros((E,), jnp.float32), 'W1': s(ks[2], (E, F, H), 0.02), 'b1': jnp.zeros((E, F), jnp.float32), 'W2': s(ks[3], (E, H, F), 0.02), 'b2': jnp.zeros((E, H), jnp.float32), 'ln_w': jnp.ones((H,), jnp.float32), 'ln_b': jnp.zeros((H,), jnp.float32)}
    _L0_ffn_in = _L0_ffn_setup()
    _d = {'L0_attn_x': _L0_attn_in['x'], 'L0_attn_Wq': _L0_attn_in['Wq'], 'L0_attn_Wk': _L0_attn_in['Wk'], 'L0_attn_Wv': _L0_attn_in['Wv'], 'L0_attn_Wo': _L0_attn_in['Wo'], 'L0_attn_W_down_kv': _L0_attn_in['W_down_kv'], 'L0_attn_W_up_k': _L0_attn_in['W_up_k'], 'L0_attn_W_up_v': _L0_attn_in['W_up_v'], 'L0_ffn_Wr': _L0_ffn_in['Wr'], 'L0_ffn_br': _L0_ffn_in['br'], 'L0_ffn_W1': _L0_ffn_in['W1'], 'L0_ffn_b1': _L0_ffn_in['b1'], 'L0_ffn_W2': _L0_ffn_in['W2'], 'L0_ffn_b2': _L0_ffn_in['b2'], 'L0_ffn_ln_w': _L0_ffn_in['ln_w'], 'L0_ffn_ln_b': _L0_ffn_in['ln_b']}
    _x0 = _d['L0_attn_x']
    _d['L0_attn_x'] = jax.random.normal(jax.random.fold_in(jax.random.key(seed), 1), (4, 512, 128), dtype=_x0.dtype)
    del _x0
    return _d

def reference(L0_attn_x, L0_attn_Wq, L0_attn_Wk, L0_attn_Wv, L0_attn_Wo, L0_attn_W_down_kv, L0_attn_W_up_k, L0_attn_W_up_v, L0_ffn_Wr, L0_ffn_br, L0_ffn_W1, L0_ffn_b1, L0_ffn_W2, L0_ffn_b2, L0_ffn_ln_w, L0_ffn_ln_b):

    def _L0_attn_ref(x, Wq, Wk, Wv, Wo, W_down_kv, W_up_k, W_up_v):
        import jax, jax.numpy as jnp
        import numpy as np
        D_MODEL = 128
        N_HEADS = 16
        HEAD_DIM = D_MODEL // N_HEADS
        D_LATENT = 32
        LAMBDA_DECAY = 0.01
        TIME_STEP = 0.01
        CLAMP = 10000.0

        def _reference_tuple_inner(x, Wq, Wk, Wv, Wo, W_down_kv, W_up_k, W_up_v):
            B, S, _ = x.shape
            q = x @ Wq
            k = x @ Wk
            v = x @ Wv
            latent_kv = (k + v) @ W_down_kv
            k_rec = latent_kv @ W_up_k
            v_rec = latent_kv @ W_up_v

            def heads(t):
                return t.reshape(B, S, N_HEADS, HEAD_DIM).transpose(0, 2, 1, 3)
            qh, kh, vh = (heads(q), heads(k_rec), heads(v_rec))
            scale = 1.0 / (jnp.sqrt(jnp.float32(D_MODEL)) + 1e-08)
            scores = jnp.einsum('bhqd,bhkd->bhqk', qh, kh) * scale
            scores = jnp.clip(jnp.nan_to_num(scores, nan=-1000000000.0), -CLAMP, CLAMP)
            idx = jnp.arange(S, dtype=jnp.float32)
            decay = jnp.exp(-LAMBDA_DECAY * TIME_STEP * jnp.abs(idx[:, None] - idx[None, :]))
            scores = scores * decay[None, None, :, :]
            scores = jnp.clip(jnp.nan_to_num(scores, nan=-1000000000.0), -CLAMP, CLAMP)
            attn = jax.nn.softmax(scores, axis=-1)
            out = jnp.einsum('bhqk,bhkd->bhqd', attn, vh)
            out = out.transpose(0, 2, 1, 3).reshape(B, S, D_MODEL)
            return (out @ Wo, latent_kv)
        return _reference_tuple_inner(x, Wq, Wk, Wv, Wo, W_down_kv, W_up_k, W_up_v)[0]

    def _L0_ffn_ref(hidden_states, Wr, br, W1, b1, W2, b2, ln_w, ln_b):
        import jax, jax.numpy as jnp
        import numpy as np
        E = 8
        TOP_K = 2
        H = 128
        F = 512
        LN_EPS = 1e-12
        bsz, seqlen, h = hidden_states.shape
        x = hidden_states.reshape(-1, h)
        logits = x @ Wr.T + br
        topk_vals, topk_idx = jax.lax.top_k(logits, TOP_K)
        topk_w = jax.nn.softmax(topk_vals, axis=-1)
        out = jnp.zeros_like(x)
        for e in range(E):
            cw = jnp.sum(topk_w * (topk_idx == e), axis=-1)
            y = jax.nn.gelu(x @ W1[e].T + b1[e], approximate=False) @ W2[e].T + b2[e]
            out = out + cw[:, None] * y
        z = out + x
        mu = jnp.mean(z, axis=-1, keepdims=True)
        var = jnp.mean(jnp.square(z - mu), axis=-1, keepdims=True)
        z = (z - mu) * jax.lax.rsqrt(var + LN_EPS) * ln_w + ln_b
        return z.reshape(bsz, seqlen, h)
    x = L0_attn_x
    xn = _layernorm(x, axis=-1)
    x = x + _L0_attn_ref(xn, L0_attn_Wq, L0_attn_Wk, L0_attn_Wv, L0_attn_Wo, L0_attn_W_down_kv, L0_attn_W_up_k, L0_attn_W_up_v) + _L0_ffn_ref(xn, L0_ffn_Wr, L0_ffn_br, L0_ffn_W1, L0_ffn_b1, L0_ffn_W2, L0_ffn_b2, L0_ffn_ln_w, L0_ffn_ln_b)
    return x

_drawn_inputs = setup_inputs


def setup_inputs(seed=0):
    import zlib

    import numpy as np

    out = dict(_drawn_inputs(seed))
    spreads = {'L0_ffn_br': (0.0, 0.1),
     'L0_ffn_b1': (0.0, 0.8),
     'L0_ffn_b2': (0.0, 0.511),
     'L0_ffn_ln_w': (1.0, 0.2),
     'L0_ffn_ln_b': (0.0, 0.323)}
    factors = {'L0_attn_Wq': 8.0,
     'L0_attn_Wk': 8.0,
     'L0_attn_Wv': 8.0,
     'L0_attn_Wo': 8.0,
     'L0_attn_W_down_kv': 8.0,
     'L0_attn_W_up_k': 8.0,
     'L0_attn_W_up_v': 8.0,
     'L0_ffn_W1': 2.927,
     'L0_ffn_W2': 2.674}
    for name, (base, spread) in spreads.items():
        noise = np.random.default_rng([zlib.crc32(name.encode()), seed]).standard_normal(out[name].shape)
        drawn = base * np.exp(spread * noise) if base else spread * noise
        out[name] = jnp.asarray(drawn.astype(out[name].dtype))
    for name, factor in factors.items():
        out[name] = (out[name] * factor).astype(out[name].dtype)
    return out
```

```python
import concourse.bass as bass
from concourse import mybir
from contextlib import ExitStack

fp32 = mybir.dt.float32
ALU = mybir.AluOpType
ACT = mybir.ActivationFunctionType
AX = mybir.AxisListType

P = 128
B, S, D = 4, 512, 128
HEADS, HD = 16, 8
LATENT = 32
EXPERTS, F = 8, 512
QT = S // P
TILES = B * QT
PAIRS = B * HEADS
FC = F // P
CLAMP = 10000.0
SCALE = 1.0 / (float(D) ** 0.5 + 1e-8)
SLOTS = 2


def build(nc, x, wq, wk, wv, wo, w_down, w_up_k, w_up_v, w_router, b_router, w1, b1, w2, b2, ln_w, ln_b,
          decay, identity, out):
    with ExitStack() as ctx:
        def sb(name, shape, dt=fp32):
            return ctx.enter_context(nc.sbuf_tensor(name, shape, dt))

        def sem(name):
            return ctx.enter_context(nc.semaphore(name))

        x_sb = sb("x_sb", [P, TILES, D])
        xn = sb("xn", [P, TILES, D])
        xnT = sb("xnT", [D, TILES * P])
        wq_sb, wk_sb, wv_sb, wo_sb = (sb(n, [D, D]) for n in ("wq_sb", "wk_sb", "wv_sb", "wo_sb"))
        wdown_sb = sb("wdown_sb", [D, LATENT])
        wup_sb = sb("wup_sb", [LATENT, 2, D])
        wkvT_sb = sb("wkvT_sb", [D, D])
        wlatT_sb = sb("wlatT_sb", [LATENT, D])
        wrec_sb = sb("wrec_sb", [D, 2, D])
        wr_sb = sb("wr_sb", [EXPERTS, D])
        wrT_sb = sb("wrT_sb", [D, EXPERTS])
        rows_sb = sb("rows_sb", [1, EXPERTS + 2 * D])
        rows_bc = sb("rows_bc", [P, EXPERTS + 2 * D])
        ones_row = sb("ones_row", [1, P])
        b1_sb = sb("b1_sb", [EXPERTS * FC, P])
        b1T_sb = sb("b1T_sb", [P, EXPERTS * FC])
        b2_sb = sb("b2_sb", [EXPERTS, D])
        w1_sb = sb("w1_sb", [P, EXPERTS * FC, D])
        w2_sb = sb("w2_sb", [D, EXPERTS * FC, P])
        w1T = sb("w1T", [D, EXPERTS * FC, P])
        w2T = sb("w2T", [P, EXPERTS * FC, D])
        decay_sb = sb("decay_sb", [P, QT, S])
        ident = sb("ident", [P, P])
        stats = sb("stats", [P, TILES, 6])
        mv = sb("mv", [P, TILES, 2])
        std = sb("std", [P, TILES])
        rstd = sb("rstd", [P, TILES])
        newton = sb("newton", [P, 3, TILES])
        logits = sb("logits", [P, TILES, EXPERTS])
        rank = sb("rank", [P, TILES, EXPERTS])
        first = sb("first", [P, TILES, EXPERTS])
        second = sb("second", [P, TILES, EXPERTS])
        pick = sb("pick", [P, TILES, EXPERTS])
        top = sb("top", [P, 8, TILES])
        cw = sb("cw", [P, TILES, EXPERTS])
        cwT = sb("cwT", [EXPERTS, TILES, P])
        qT_sb = sb("qT_sb", [D, TILES * P])
        kT_sb = sb("kT_sb", [D, TILES * P])
        v_sb = sb("v_sb", [P, PAIRS, QT, HD])
        attn = sb("attn", [P, QT, PAIRS, HD])
        q_head = sb("q_head", [HD, SLOTS, S])
        k_head = sb("k_head", [HD, SLOTS, S])
        clipped = sb("clipped", [P, SLOTS, S])
        decayed = sb("decayed", [P, SLOTS, S])
        row_max = sb("row_max", [P, SLOTS])
        neg_max = sb("neg_max", [P, SLOTS])
        probs = sb("probs", [P, SLOTS, S])
        row_sum = sb("row_sum", [P, SLOTS])
        inv_sum = sb("inv_sum", [P, SLOTS])
        probsT = sb("probsT", [P, SLOTS, S])
        hidden = sb("hidden", [P, 2, FC, S])
        acc = sb("acc", [P, TILES, D])
        attnT = sb("attnT", [D, TILES, P])
        z = qT_sb[:].rearrange("p (t d) -> p t d", t=TILES)

        ps = ctx.enter_context(nc.psum_tensor("ps", [P, 8, 512], fp32))
        q_scr = nc.dram_tensor("q_scr", (PAIRS, HD, S), fp32, kind="Internal").ap()
        k_scr = nc.dram_tensor("k_scr", (PAIRS, HD, S), fp32, kind="Internal").ap()

        x_in = [sem(f"x_in{b}") for b in range(B)]
        small_in, w1_in, w2_in, decay_in = sem("small_in"), sem("w1_in"), sem("w2_in"), sem("decay_in")
        scratch_out, stored = sem("scratch_out"), sem("stored")
        head_in = [sem(f"head_in{u}") for u in range(SLOTS)]
        dve = sem("dve_step")
        ones_set, kv_sum, var_ready, std_ready, xn_ready = (
            sem(n) for n in ("ones_set", "kv_sum", "var_ready", "std_ready", "xn_ready"))
        prep_psum, prep_copied = sem("prep_psum"), sem("prep_copied")
        xnT_psum, xnT_ready = sem("xnT_psum"), sem("xnT_ready")
        wT_psum, wT_ready = sem("wT_psum"), sem("wT_ready")
        proj_psum, qk_ready, v_ready, logits_ready = (
            sem(n) for n in ("proj_psum", "qk_ready", "v_ready", "logits_ready"))
        gap_ready, gap_exp = sem("gap_ready"), sem("gap_exp")
        scores_ready, scores_read, max_ready, probs_ready = (
            sem(n) for n in ("scores_ready", "scores_read", "max_ready", "probs_ready"))
        probsT_psum, probsT_ready, attn_psum, attn_read = (
            sem(n) for n in ("probsT_psum", "probsT_ready", "attn_psum", "attn_read"))
        cw_ready, cwT_psum, cwT_ready, bias_psum, acc_ready = (
            sem(n) for n in ("cw_ready", "cwT_psum", "cwT_ready", "bias_psum", "acc_ready"))
        hidden_psum, hidden_ready, y_psum, y_read = (
            sem(n) for n in ("hidden_psum", "hidden_ready", "y_psum", "y_read"))
        attnT_psum, attnT_ready, wo_psum, z_var, z_std, out_ready = (
            sem(n) for n in ("attnT_psum", "attnT_ready", "wo_psum", "z_var", "z_std", "out_ready"))

        SMALL = 15
        w_groups = 2 * EXPERTS

        def head_rows(ap, b):
            return ap[:, b * S:(b + 1) * S]

        block = ctx.enter_context(nc.Block())

        @block.sync
        def _(sp):
            for b in range(B):
                sp.dma_start(x_sb[:, b * QT:(b + 1) * QT, :],
                             x[b].rearrange("(t p) d -> p t d", p=P)).then_inc(x_in[b], 16)
            for dst, src in ((ident[:], identity), (wk_sb[:], wk), (wv_sb[:], wv), (wq_sb[:], wq),
                             (wdown_sb[:], w_down), (wup_sb[:, 0, :], w_up_k), (wup_sb[:, 1, :], w_up_v),
                             (wr_sb[:], w_router), (wo_sb[:], wo),
                             (b1_sb[:], b1.rearrange("e (c p) -> (e c) p", p=P)), (b2_sb[:], b2),
                             (rows_sb[0:1, 0:EXPERTS], b_router.rearrange("(a n) -> a n", a=1)),
                             (rows_sb[0:1, EXPERTS:EXPERTS + D], ln_w.rearrange("(a n) -> a n", a=1)),
                             (rows_sb[0:1, EXPERTS + D:], ln_b.rearrange("(a n) -> a n", a=1))):
                sp.dma_start(dst, src).then_inc(small_in, 16)
            sp.dma_start(decay_sb[:], decay.rearrange("(t p) k -> p t k", p=P)).then_inc(decay_in, 16)
            sp.dma_start(w1_sb[:], w1.rearrange("e (c p) h -> p (e c) h", p=P)).then_inc(w1_in, 16)
            sp.dma_start(w2_sb[:].rearrange("p (e c) f -> p e (c f)", c=FC),
                         w2.rearrange("e h f -> h e f")).then_inc(w2_in, 16)
            sp.wait_ge(qk_ready, 2 * B)
            for sc, src in ((q_scr, qT_sb), (k_scr, kT_sb)):
                for b in range(B):
                    sp.dma_start(sc[b * HEADS:(b + 1) * HEADS].rearrange("h d s -> (h d) s"),
                                 head_rows(src, b)).then_inc(scratch_out, 16)
            sp.wait_ge(scratch_out, 2 * B * 16)

            def load_head(pair, u):
                sp.dma_start(q_head[:, u:u + 1, :], q_scr[bass.ds(pair, 1)].rearrange("a d s -> d a s")).then_inc(head_in[u], 16)
                sp.dma_start(k_head[:, u:u + 1, :], k_scr[bass.ds(pair, 1)].rearrange("a d s -> d a s")).then_inc(head_in[u], 16)

            for u in range(SLOTS):
                load_head(u, u)
            with sp.Fori(0, PAIRS // SLOTS - 1) as m:
                n = m * SLOTS
                for u in range(SLOTS):
                    sp.wait_ge(scores_ready, (n + (u + 1)) * QT)
                    load_head(n + (SLOTS + u), u)
            for t in range(TILES):
                sp.wait_ge(out_ready, t + 1)
                sp.dma_start(out[t // QT, (t % QT) * P:(t % QT + 1) * P, :], z[:, t, :]).then_inc(stored, 16)
            sp.wait_ge(stored, TILES * 16)

        @block.tensor
        def _(pe):
            pe.wait_ge(small_in, 14 * 16)
            pe.wait_ge(ones_set, 1)
            nc.tensor.transpose(ps[:, 0, 0:EXPERTS], wr_sb[:], ident[0:EXPERTS, 0:EXPERTS])
            nc.tensor.transpose(ps[:, 0, 8:40], b1_sb[:], ident[0:32, 0:32]).then_inc(prep_psum, 1)
            nc.tensor.matmul(ps[:, 1, 0:EXPERTS + 2 * D], ones_row[:], rows_sb[:], start=True, stop=True).then_inc(prep_psum, 1)
            pe.wait_ge(kv_sum, 1)
            nc.tensor.transpose(ps[:, 2, 0:D], wk_sb[:], ident[:]).then_inc(prep_psum, 1)
            pe.wait_ge(prep_copied, 3)
            nc.tensor.matmul(ps[0:LATENT, 3, 0:D], wdown_sb[:], wkvT_sb[:], start=True, stop=True).then_inc(prep_psum, 1)
            pe.wait_ge(prep_copied, 4)
            nc.tensor.matmul(ps[:, 4, 0:2 * D], wlatT_sb[:], wup_sb[:].rearrange("l a d -> l (a d)"),
                             start=True, stop=True).then_inc(prep_psum, 1)
            pe.wait_ge(prep_copied, 5)
            for b in range(B):
                pe.wait_ge(xn_ready, (b + 1) * QT)
                for t in range(QT):
                    last = nc.tensor.transpose(ps[:, b, t * P:(t + 1) * P], xn[:, b * QT + t, :], ident[:])
                last.then_inc(xnT_psum, 1)
            for b in range(B):
                tok = slice(b * S, (b + 1) * S)
                pe.wait_ge(xnT_ready, b + 1)
                if b:
                    pe.wait_ge(qk_ready, 2 * b)
                    pe.wait_ge(v_ready, b)
                    pe.wait_ge(logits_ready, b)
                nc.tensor.matmul(ps[:, 4, :], wq_sb[:], xnT[:, tok], start=True, stop=True)
                nc.tensor.matmul(ps[:, 5, :], wrec_sb[:, 0, :], xnT[:, tok], start=True, stop=True)
                for t in range(QT):
                    tile = xnT[:, (b * QT + t) * P:(b * QT + t + 1) * P]
                    nc.tensor.matmul(ps[:, 6, t * D:(t + 1) * D], tile, wrec_sb[:, 1, :], start=True, stop=True)
                for t in range(QT):
                    tile = xnT[:, (b * QT + t) * P:(b * QT + t + 1) * P]
                    last = nc.tensor.matmul(ps[:, 7, t * EXPERTS:(t + 1) * EXPERTS], tile, wrT_sb[:], start=True, stop=True)
                last.then_inc(proj_psum, 1)
            for g in range(w_groups):
                src, loaded = (w1_sb, w1_in) if g < EXPERTS else (w2_sb, w2_in)
                pe.wait_ge(loaded, 16)
                if g >= 4:
                    pe.wait_ge(wT_ready, g - 3)
                for c in range(FC):
                    last = nc.tensor.transpose(ps[:, g % 4, c * P:(c + 1) * P],
                                               src[:, (g % EXPERTS) * FC + c, :], ident[:])
                last.then_inc(wT_psum, 1)
            pe.wait_ge(wT_ready, w_groups)
            pe.wait_ge(qk_ready, 2 * B)
            pe.wait_ge(v_ready, B)

            def scores(pair, u, t):
                s = t % SLOTS
                nc.tensor.matmul(ps[:, s, :], q_head[:, u, t * P:(t + 1) * P], k_head[:, u, :],
                                 start=True, stop=True).then_inc(scores_ready, 1)

            def transposes(s):
                for k in range(QT):
                    last = nc.tensor.transpose(ps[:, 2 + s, k * P:(k + 1) * P], probs[:, s, k * P:(k + 1) * P], ident[:])
                last.then_inc(probsT_psum, 1)

            def outputs(pair, s):
                for k in range(QT):
                    last = nc.tensor.matmul(ps[:, 4 + s, 0:HD], probsT[:, s, k * P:(k + 1) * P],
                                            v_sb[:, bass.ds(pair, 1), k, :], start=(k == 0), stop=(k == QT - 1))
                last.then_inc(attn_psum, 1)

            with pe.Fori(0, PAIRS // SLOTS) as m:
                n = m * SLOTS
                for u in range(SLOTS):
                    pe.wait_ge(head_in[u], (n * 16 + 32))
                    for t in range(QT):
                        s = t % SLOTS
                        step = (n + u) * QT + t
                        if u or t >= SLOTS:
                            pe.wait_ge(scores_read, step - 1)
                        else:
                            pe.wait_ge(scores_read, (n + u) * QT + (t - t % SLOTS))
                        scores(n + u, u, t)
                        pe.wait_ge(probs_ready, step + 1)
                        transposes(s)
                        pe.wait_ge(probsT_ready, step + 1)
                        outputs(n + u, s)
            pe.wait_ge(cw_ready, 1)
            pe.wait_ge(attn_read, PAIRS * QT)
            for g in range(4):
                for t in range(4):
                    last = nc.tensor.transpose(ps[0:EXPERTS, g, t * P:(t + 1) * P], cw[:, g * 4 + t, :], ident[:])
            last.then_inc(cwT_psum, 1)
            pe.wait_ge(cwT_ready, 1)
            for g in range(4):
                for t in range(4):
                    last = nc.tensor.matmul(ps[:, g, t * D:(t + 1) * D], cwT[:, g * 4 + t, :], b2_sb[:], start=True, stop=True)
            last.then_inc(bias_psum, 1)
            pe.wait_ge(acc_ready, 1)

            with pe.Fori(0, B) as b:
                for e in range(EXPERTS):
                    for c in range(FC):
                        pe.wait_ge(hidden_ready, b * (EXPERTS * FC) + max(e - 1, 0) * FC + (c + 1 if e else 0))
                        nc.tensor.matmul(ps[:, c, :], w1T[:, e * FC + c, :], xnT[:, bass.ds(b * S, S)],
                                         start=True, stop=True).then_inc(hidden_psum, 1)
                    pe.wait_ge(hidden_ready, b * (EXPERTS * FC) + (e + 1) * FC)
                    pe.wait_ge(y_read, b * EXPERTS + max(e - 1, 0))
                    for c in range(FC):
                        for t in range(QT):
                            last = nc.tensor.matmul(ps[:, 4 + e % 2, t * D:(t + 1) * D],
                                                    hidden[:, e % 2, c, t * P:(t + 1) * P], w2T[:, e * FC + c, :],
                                                    start=(c == 0 and t == 0), stop=(c == FC - 1 and t == QT - 1),
                                                    skip_group_check=True)
                    last.then_inc(y_psum, 1)
            for b in range(B):
                for t in range(QT):
                    last = nc.tensor.transpose(ps[:, b, t * P:(t + 1) * P],
                                               attn[:, t, b * HEADS:(b + 1) * HEADS, :].rearrange("p h d -> p (h d)"), ident[:])
                last.then_inc(attnT_psum, 1)
            pe.wait_ge(y_read, B * EXPERTS)
            for b in range(B):
                pe.wait_ge(attnT_ready, b + 1)
                for t in range(QT):
                    last = nc.tensor.matmul(ps[:, 4 + b, t * D:(t + 1) * D], attnT[:, b * QT + t, :], wo_sb[:],
                                            start=True, stop=True)
                last.then_inc(wo_psum, 1)

        @block.scalar
        def _(act):
            act.wait_ge(var_ready, 1)
            nc.scalar.activation(std[:], newton[:, 0, :], ACT.Sqrt).then_inc(std_ready, 1)
            for b in range(B):
                act.wait_ge(xnT_psum, b + 1)
                nc.scalar.copy(xnT[:, b * S:(b + 1) * S], ps[:, b, :]).then_inc(xnT_ready, 1)
            for b in range(B):
                tok = slice(b * S, (b + 1) * S)
                act.wait_ge(proj_psum, b + 1)
                nc.scalar.mul(qT_sb[:, tok], ps[:, 4, :], SCALE).then_inc(qk_ready, 1)
                nc.scalar.copy(kT_sb[:, tok], ps[:, 5, :]).then_inc(qk_ready, 1)
            for g in range(0, w_groups):
                dst = w1T if g < EXPERTS else w2T
                act.wait_ge(wT_psum, g + 1)
                nc.scalar.copy(dst[:, (g % EXPERTS) * FC:(g % EXPERTS + 1) * FC, :],
                               ps[:, g % 4, :].rearrange("p (c f) -> p c f", c=FC)).then_inc(wT_ready, 1)
            act.wait_ge(gap_ready, 1)
            nc.scalar.activation(top[:, 5, :], top[:, 4, :], ACT.Exp).then_inc(gap_exp, 1)
            with act.Fori(0, PAIRS) as n:
                for t in range(QT):
                    s = t % SLOTS
                    step = n * QT + t
                    act.wait_ge(max_ready, step + 1)
                    nc.scalar.activation(probs[:, s, :], decayed[:, s, :], ACT.Exp, bias=neg_max[:, s:s + 1],
                                         accum_out=row_sum[:, s:s + 1]).then_inc(probs_ready, 1)
                    act.wait_ge(probsT_psum, step + 1)
                    nc.scalar.copy(probsT[:, s, :], ps[:, 2 + s, :]).then_inc(probsT_ready, 1)
            with act.Fori(0, B) as b:
                for e in range(EXPERTS):
                    act.wait_ge(y_psum, b * EXPERTS + max(e - 1, 0))
                    for c in range(FC):
                        act.wait_ge(hidden_psum, b * (EXPERTS * FC) + (e * FC + c + 1))
                        nc.scalar.activation(hidden[:, e % 2, c, :], ps[:, c, :], ACT.Gelu,
                                             bias=b1T_sb[:, e * FC + c:e * FC + c + 1]).then_inc(hidden_ready, 1)
            for b in range(B):
                act.wait_ge(attnT_psum, b + 1)
                nc.scalar.copy(attnT[:, b * QT:(b + 1) * QT, :], ps[:, b, :].rearrange("p (t f) -> p t f", t=QT)).then_inc(attnT_ready, 1)
            act.wait_ge(z_var, 1)
            nc.scalar.activation(std[:], newton[:, 0, :], ACT.Sqrt).then_inc(z_std, 1)

        @block.vector
        def _(v):
            steps = [0]

            def then(ins, n=1):
                steps[0] += 1
                ins.then_inc(dve, 1)
                v.wait_ge(dve, steps[0])

            def refine_rstd(var, eps, waits, signal, done):
                then(nc.vector.tensor_scalar(newton[:, 0, :], var, eps, None, ALU.add))
                nc.vector.tensor_copy(newton[:, 1, :], newton[:, 0, :]).then_inc(signal, 1)
                v.wait_ge(done, 1)
                then(nc.vector.reciprocal(rstd[:], std[:]))
                then(nc.vector.tensor_tensor(newton[:, 2, :], rstd[:], rstd[:], ALU.mult))
                then(nc.vector.tensor_tensor(newton[:, 2, :], newton[:, 2, :], newton[:, 0, :], ALU.mult))
                then(nc.vector.tensor_scalar(newton[:, 2, :], newton[:, 2, :], -0.5, 1.5, ALU.mult, ALU.add))
                then(nc.vector.tensor_tensor(rstd[:], rstd[:], newton[:, 2, :], ALU.mult))

            nc.vector.memset(ones_row[:], 1.0).then_inc(ones_set, 1)
            for e in range(EXPERTS):
                last = nc.vector.memset(rank[:, :, e:e + 1], float(EXPERTS - e))
            then(last)
            for b in range(B):
                v.wait_ge(x_in[b], 16)
                for t in range(b * QT, (b + 1) * QT):
                    last = nc.vector.bn_stats(stats[:, t, :], x_sb[:, t, :])
            then(last)
            for t in range(TILES):
                last = nc.vector.bn_aggr(mv[:, t, :], stats[:, t, :])
            then(last)
            refine_rstd(mv[:, :, 1], 1e-5, None, var_ready, std_ready)
            for t in range(TILES):
                nc.vector.tensor_scalar(xn[:, t, :], x_sb[:, t, :], mv[:, t, 0:1], rstd[:, t:t + 1],
                                        ALU.subtract, ALU.mult).then_inc(xn_ready, 1)
            v.wait_ge(small_in, 14 * 16)
            nc.vector.tensor_tensor(wk_sb[:], wk_sb[:], wv_sb[:], ALU.add).then_inc(kv_sum, 1)
            v.wait_ge(prep_psum, 1)
            nc.vector.tensor_copy(wrT_sb[:], ps[:, 0, 0:EXPERTS])
            nc.vector.tensor_copy(b1T_sb[:], ps[:, 0, 8:40]).then_inc(prep_copied, 1)
            v.wait_ge(prep_psum, 2)
            nc.vector.tensor_copy(rows_bc[:], ps[:, 1, 0:EXPERTS + 2 * D]).then_inc(prep_copied, 1)
            v.wait_ge(prep_psum, 3)
            nc.vector.tensor_copy(wkvT_sb[:], ps[:, 2, 0:D]).then_inc(prep_copied, 1)
            v.wait_ge(prep_psum, 4)
            nc.vector.tensor_copy(wlatT_sb[:], ps[0:LATENT, 3, 0:D]).then_inc(prep_copied, 1)
            v.wait_ge(prep_psum, 5)
            nc.vector.tensor_copy(wrec_sb[:], ps[:, 4, 0:2 * D].rearrange("p (a d) -> p a d", a=2)).then_inc(prep_copied, 1)
            for b in range(B):
                v.wait_ge(proj_psum, b + 1)
                nc.vector.tensor_copy(v_sb[:, b * HEADS:(b + 1) * HEADS, :, :],
                                      ps[:, 6, :].rearrange("p (k h d) -> p h k d", k=QT, h=HEADS)).then_inc(v_ready, 1)
                nc.vector.tensor_tensor(logits[:, b * QT:(b + 1) * QT, :],
                                        ps[:, 7, 0:QT * EXPERTS].rearrange("p (t e) -> p t e", t=QT),
                                        rows_bc[:, None, 0:EXPERTS].to_broadcast([P, QT, EXPERTS]), ALU.add).then_inc(logits_ready, 1)
            v.wait_ge(logits_ready, B)

            def top_one(values, largest, onehot):
                ranks = top[:, 2, :]
                then(nc.vector.tensor_reduce(largest, values, AX.X, ALU.max))
                then(nc.vector.tensor_tensor(pick[:], values, largest.unsqueeze(2).to_broadcast([P, TILES, EXPERTS]), ALU.is_equal))
                then(nc.vector.tensor_tensor(pick[:], pick[:], rank[:], ALU.mult))
                then(nc.vector.tensor_reduce(ranks, pick[:], AX.X, ALU.max))
                then(nc.vector.tensor_tensor(onehot, rank[:], ranks.unsqueeze(2).to_broadcast([P, TILES, EXPERTS]), ALU.is_equal))

            top_one(logits[:], top[:, 0, :], first[:])
            then(nc.vector.scalar_tensor_tensor(logits[:], first[:], -3.0e38, logits[:], ALU.mult, ALU.add))
            top_one(logits[:], top[:, 1, :], second[:])
            nc.vector.tensor_tensor(top[:, 4, :], top[:, 1, :], top[:, 0, :], ALU.subtract).then_inc(gap_ready, 1)
            v.wait_ge(gap_exp, 1)
            then(nc.vector.tensor_scalar(top[:, 6, :], top[:, 5, :], 1.0, None, ALU.add))
            then(nc.vector.reciprocal(top[:, 6, :], top[:, 6, :]))
            then(nc.vector.tensor_tensor(top[:, 7, :], top[:, 5, :], top[:, 6, :], ALU.mult))
            then(nc.vector.tensor_tensor(first[:], first[:], top[:, 6, :].unsqueeze(2).to_broadcast([P, TILES, EXPERTS]), ALU.mult))
            then(nc.vector.tensor_tensor(second[:], second[:], top[:, 7, :].unsqueeze(2).to_broadcast([P, TILES, EXPERTS]), ALU.mult))
            nc.vector.tensor_tensor(cw[:], first[:], second[:], ALU.add).then_inc(cw_ready, 1)

            v.wait_ge(decay_in, 16)
            base = steps[0]
            LOOP = 3
            with v.Fori(0, PAIRS) as n:
                for t in range(QT):
                    s = t % SLOTS
                    step = n * QT + t
                    v.wait_ge(scores_ready, step + 1)
                    nc.vector.tensor_scalar(clipped[:, s, :], ps[:, s, :], CLAMP, -CLAMP, ALU.min, ALU.max).then_inc(scores_read, 1)
                    v.wait_ge(scores_read, step + 1)
                    v.wait_ge(probs_ready, n * QT + max(t - 1, 0))
                    nc.vector.tensor_tensor(decayed[:, s, :], clipped[:, s, :], decay_sb[:, t, :], ALU.mult).then_inc(dve, 1)
                    v.wait_ge(dve, step * LOOP + (base + 1))
                    nc.vector.tensor_reduce(row_max[:, s:s + 1], decayed[:, s, :], AX.X, ALU.max).then_inc(dve, 1)
                    v.wait_ge(dve, step * LOOP + (base + 2))
                    nc.vector.tensor_scalar(neg_max[:, s:s + 1], row_max[:, s:s + 1], -1.0, None, ALU.mult).then_inc(max_ready, 1)
                    v.wait_ge(probs_ready, step + 1)
                    nc.vector.reciprocal(inv_sum[:, s:s + 1], row_sum[:, s:s + 1]).then_inc(dve, 1)
                    v.wait_ge(dve, step * LOOP + (base + 3))
                    v.wait_ge(attn_psum, step + 1)
                    nc.vector.tensor_scalar(attn[:, t, bass.ds(n, 1), :], ps[:, 4 + s, 0:HD].unsqueeze(1), inv_sum[:, s:s + 1], None,
                                            ALU.mult).then_inc(attn_read, 1)
            steps[0] = base + LOOP * PAIRS * QT
            v.wait_ge(cwT_psum, 1)
            then(nc.vector.tensor_copy(cwT[:].rearrange("e t p -> e (t p)"), ps[0:EXPERTS, 0:4, :].rearrange("e g p -> e (g p)")))
            nc.vector.tensor_copy(top[:, 3, :], top[:, 2, :]).then_inc(cwT_ready, 1)
            v.wait_ge(bias_psum, 1)
            nc.vector.tensor_tensor(acc[:], ps[:, 0:4, :].rearrange("p g (t d) -> p (g t) d", t=4), xn[:], ALU.add).then_inc(acc_ready, 1)
            v.wait_ge(acc_ready, 1)
            with v.Fori(0, B) as b:
                for e in range(EXPERTS):
                    v.wait_ge(y_psum, b * EXPERTS + (e + 1))
                    v.wait_ge(y_read, b * EXPERTS + e)
                    for t in range(QT):
                        tile = acc[:, bass.ds(b * QT + t, 1), :]
                        last = nc.vector.scalar_tensor_tensor(
                            tile, ps[:, 4 + e % 2, t * D:(t + 1) * D], cw[:, bass.ds(b * QT + t, 1), e], tile,
                            ALU.mult, ALU.add)
                    last.then_inc(y_read, 1)
            v.wait_ge(y_read, B * EXPERTS)
            for t in range(TILES):
                last = nc.vector.bn_stats(stats[:, t, :], acc[:, t, :])
            then(last)
            for t in range(TILES):
                last = nc.vector.bn_aggr(mv[:, t, :], stats[:, t, :])
            then(last)
            refine_rstd(mv[:, :, 1], 1e-12, None, z_var, z_std)
            for t in range(TILES):
                last = nc.vector.tensor_scalar(z[:, t, :], acc[:, t, :], mv[:, t, 0:1], rstd[:, t:t + 1],
                                               ALU.subtract, ALU.mult)
            then(last)
            wide = lambda a: rows_bc[:, None, EXPERTS + a * D:EXPERTS + (a + 1) * D].to_broadcast([P, TILES, D])
            then(nc.vector.tensor_tensor(z, z, wide(0), ALU.mult))
            then(nc.vector.tensor_tensor(z, z, wide(1), ALU.add))
            then(nc.vector.tensor_tensor(z, z, x_sb[:], ALU.add))
            v.wait_ge(wo_psum, B)
            for t in range(TILES):
                nc.vector.tensor_tensor(z[:, t, :], ps[:, 4 + t // QT, (t % QT) * D:(t % QT + 1) * D], z[:, t, :],
                                        ALU.add).then_inc(out_ready, 1)


NAMES = ["L0_attn_x", "L0_attn_Wq", "L0_attn_Wk", "L0_attn_Wv", "L0_attn_Wo", "L0_attn_W_down_kv",
         "L0_attn_W_up_k", "L0_attn_W_up_v", "L0_ffn_Wr", "L0_ffn_br", "L0_ffn_W1", "L0_ffn_b1",
         "L0_ffn_W2", "L0_ffn_b2", "L0_ffn_ln_w", "L0_ffn_ln_b"]


def kernel(**inputs):
    import numpy as np
    import concourse.bacc as bacc
    from concourse.bass_utils import run_bass_kernel_spmd

    nc = bacc.Bacc("TRN2", target_bir_lowering=False, num_devices=1)
    arrays = {name: np.ascontiguousarray(inputs[name]) for name in NAMES}
    at = np.arange(S, dtype=np.float32)
    arrays["decay"] = np.exp(np.float32(-0.01 * 0.01) * np.abs(at[:, None] - at[None, :])).astype(np.float32)
    arrays["identity"] = np.eye(P, dtype=np.float32)
    aps = [nc.dram_tensor(n, a.shape, mybir.dt.from_np(a.dtype), kind="ExternalInput").ap() for n, a in arrays.items()]
    out = nc.dram_tensor("out", (B, S, D), fp32, kind="ExternalOutput").ap()
    build(nc, *aps, out)
    result = run_bass_kernel_spmd(nc, [arrays], core_ids=[0])
    return result.results[0]["out"]
```

```python
import concourse.bass as bass
from concourse import mybir
from contextlib import ExitStack

fp32 = mybir.dt.float32
bf16 = mybir.dt.bfloat16
i32 = mybir.dt.int32
ALU = mybir.AluOpType
ACT = mybir.ActivationFunctionType
AX = mybir.AxisListType

P = 128
B, S, D = 4, 512, 128
HEADS, HD = 16, 8
LATENT = 32
EXPERTS, F = 8, 512
QT = S // P
TILES = B * QT
PAIRS = B * HEADS
FC = F // P
CLAMP = 10000.0
SCALE = 1.0 / (float(D) ** 0.5 + 1e-8)
SLOTS = 2
SAFE = 64.0
GROUP = 4
GROUPS = PAIRS // GROUP
UNITS = 2 * PAIRS
QUADS = UNITS // GROUP
PARTS = 3
PRODUCTS = [(0, 0), (0, 1), (1, 0), (0, 2), (2, 0), (1, 1)]
VW = HD + 1


def build(nc, x, wq, wk, wv, wo, w_down, w_up_k, w_up_v, w_router, b_router, w1, b1, w2, b2, ln_w, ln_b,
          decay, identity, fold, mend, head_ones, out):
    with ExitStack() as ctx:
        def sb(name, shape, dt=fp32):
            return ctx.enter_context(nc.sbuf_tensor(name, shape, dt))

        def sem(name):
            return ctx.enter_context(nc.semaphore(name))

        x_sb = sb("x_sb", [P, TILES, D])
        xn = x_sb
        xnT = sb("xnT", [D, TILES * P])
        wq_sb, wk_sb, wv_sb, wo_sb = (sb(n, [D, D]) for n in ("wq_sb", "wk_sb", "wv_sb", "wo_sb"))
        wq_cols = sb("wq_cols", [D, D])
        wdown_sb = sb("wdown_sb", [D, LATENT])
        wup_sb = sb("wup_sb", [LATENT, 2, D])
        wkvT_sb = sb("wkvT_sb", [D, D])
        wlatT_sb = sb("wlatT_sb", [LATENT, D])
        wrec_sb = sb("wrec_sb", [D, 2, D])
        wr_sb = sb("wr_sb", [EXPERTS, D])
        wrT_sb = sb("wrT_sb", [D, EXPERTS])
        rows_sb = sb("rows_sb", [1, EXPERTS + 2 * D])
        rows_bc = sb("rows_bc", [P, EXPERTS + 2 * D])
        ones_row = sb("ones_row", [1, P])
        b1_sb = sb("b1_sb", [EXPERTS * FC, P])
        b1T_sb = sb("b1T_sb", [P, EXPERTS * FC])
        b2_sb = sb("b2_sb", [EXPERTS, D])
        w_raw = sb("w_raw", [P, 2, EXPERTS * FC, P])
        w1_sb, w2_sb = w_raw[:, 0], w_raw[:, 1]
        probs_fast = w_raw[:].rearrange("p a b c -> p (a b c)").rearrange("p (q g n) -> p q g n", q=2, g=GROUP)
        w1T = sb("w1T", [D, EXPERTS * FC, P])
        w2T = sb("w2T", [P, EXPERTS * FC, D])
        ident = sb("ident", [P, P])
        stats = sb("stats", [P, TILES, 6])
        mv = sb("mv", [P, TILES, 2])
        std = sb("std", [P, TILES])
        rstd = sb("rstd", [P, TILES])
        newton = sb("newton", [P, 3, TILES])
        logits = sb("logits", [P, TILES, EXPERTS])
        rank = sb("rank", [P, TILES, EXPERTS])
        first = sb("first", [P, TILES, EXPERTS])
        second = sb("second", [P, TILES, EXPERTS])
        pick = sb("pick", [P, TILES, EXPERTS])
        top = sb("top", [P, 8, TILES])
        cw = sb("cw", [P, TILES, EXPERTS])
        qT_sb = sb("qT_sb", [D, TILES * P])
        kT_sb = sb("kT_sb", [D, TILES * P])
        v_sb = sb("v_sb", [P, TILES, HEADS, VW])
        attn = qT_sb[:].rearrange("p (t h d) -> p t h d", t=TILES, h=HEADS)
        fold_sb = sb("fold_sb", [P, 2, S])
        mend_sb = [sb(f"mend_sb{half}", [P, 2, (2 * half + 2) * P]) for half in range(2)]
        ones_f = sb("ones_f", [P, HEADS])
        ones_b = sb("ones_b", [P, HEADS], bf16)
        squares = sb("squares", [P, 2, S], bf16)
        square_sums = sb("square_sums", [P, 2 * B])
        finite = sb("finite", [P, 2 * B])
        all_finite = sb("all_finite", [P, 1])
        norm_max = sb("norm_max", [HEADS, B, 2])
        bound = sb("bound", [HEADS, B])
        bound_max = sb("bound_max", [HEADS, 1])
        verdict = sb("verdict", [1, 4])
        flag = sb("flag", [1, 1], i32)
        folded = sb("folded", [P, S])
        parts = sb("parts", [P, 2, PARTS, S], bf16)
        out_heads = sb("out_heads", [P, S])
        inv_fast = sb("inv_fast", [P, QT, GROUP, 1])
        stacked = sb("stacked", [P, 2, 2, HEADS, S], bf16)
        q_rows, k_rows = stacked[:, 0], stacked[:, 1]
        words = stacked[:].rearrange("p a b h s -> p (a b h s)").bitcast(fp32)
        spot = [0]

        def over(n, size, part=P):
            a = words[0:part, spot[0]:spot[0] + n * size].rearrange("p (n s) -> p n s", n=n)
            spot[0] += n * size
            return a

        decay_sb = over(QT, S)
        q_head, k_head = over(SLOTS, S, HD), over(SLOTS, S, HD)
        clipped, decayed, probs, probsT = (over(SLOTS, S) for _ in range(4))
        spot[0] = 0
        hidden = over(2 * FC, S).rearrange("p (a c) s -> p a c s", a=2)
        cwT = over(TILES, P, EXPERTS)
        x_again = over(TILES, D)
        z = over(TILES, D)
        row_max = sb("row_max", [P, SLOTS])
        neg_max = sb("neg_max", [P, SLOTS])
        row_sum = sb("row_sum", [P, SLOTS])
        inv_sum = sb("inv_sum", [P, SLOTS])
        acc = xn
        attnT = kT_sb[:].rearrange("p (t f) -> p t f", t=TILES)

        ps = ctx.enter_context(nc.psum_tensor("ps", [P, 8, 512], fp32))
        q_scr = nc.dram_tensor("q_scr", (PAIRS, HD, S), fp32, kind="Internal").ap()
        k_scr = nc.dram_tensor("k_scr", (PAIRS, HD, S), fp32, kind="Internal").ap()

        x_in = [sem(f"x_in{b}") for b in range(B)]
        small_in, w1_in, w2_in, decay_in = sem("small_in"), sem("w1_in"), sem("w2_in"), sem("decay_in")
        scratch_out, stored = sem("scratch_out"), sem("stored")
        head_in = [sem(f"head_in{u}") for u in range(SLOTS)]
        dve, gen_step = sem("dve_step"), sem("gen_step")
        ones_set, kv_sum, var_ready, std_ready, xn_ready = (
            sem(n) for n in ("ones_set", "kv_sum", "var_ready", "std_ready", "xn_ready"))
        prep_psum, prep_copied = sem("prep_psum"), sem("prep_copied")
        xnT_psum, xnT_ready = sem("xnT_psum"), sem("xnT_ready")
        wT_psum, wT_ready = sem("wT_psum"), sem("wT_ready")
        proj_psum, qk_ready, v_ready, logits_ready = (
            sem(n) for n in ("proj_psum", "qk_ready", "v_ready", "logits_ready"))
        gap_ready, gap_exp = sem("gap_ready"), sem("gap_exp")
        scores_ready, scores_read, max_ready, probs_ready = (
            sem(n) for n in ("scores_ready", "scores_read", "max_ready", "probs_ready"))
        probsT_psum, probsT_ready, attn_psum, attn_read = (
            sem(n) for n in ("probsT_psum", "probsT_ready", "attn_psum", "attn_read"))
        cw_ready, cwT_psum, cwT_ready, bias_psum, acc_ready = (
            sem(n) for n in ("cw_ready", "cwT_psum", "cwT_ready", "bias_psum", "acc_ready"))
        x_back = sem("x_back")
        const_in, zeroed, v_ones = sem("const_in"), sem("zeroed"), sem("v_ones")
        squares_ready, norms_psum, norms_read, checks_ready, checks_psum, flag_ready = (
            sem(n) for n in ("squares_ready", "norms_psum", "norms_read", "checks_ready", "checks_psum", "flag_ready"))
        parts_ready = sem("parts_ready")
        rows_in = [sem(f"rows_in{u}") for u in range(2)]
        pool_step = sem("pool_step")
        fast_scores, fast_fixed, fast_probs, fast_used, fast_out, fast_heads, fast_outT, fast_done = (
            sem(n) for n in ("fast_scores", "fast_fixed", "fast_probs", "fast_used", "fast_out", "fast_heads",
                             "fast_outT", "fast_done"))
        fast_step, after_step = sem("fast_step"), sem("after_step")
        hidden_psum, hidden_ready, y_psum, y_read = (
            sem(n) for n in ("hidden_psum", "hidden_ready", "y_psum", "y_read"))
        attnT_psum, attnT_ready, wo_psum, z_var, z_std, out_ready = (
            sem(n) for n in ("attnT_psum", "attnT_ready", "wo_psum", "z_var", "z_std", "out_ready"))

        w_groups = 2 * EXPERTS

        def head_rows(ap, b):
            return ap[:, b * S:(b + 1) * S]

        def split(eng, waiter, then, b, sides):
            waiter.wait_ge(const_in, 48)
            for side in sides:
                kept = (qT_sb, kT_sb)[side]
                buf = folded[:]
                waiter.wait_ge(qk_ready, 2 * b + side + 1)
                if b:
                    waiter.wait_ge(rows_in[(b - 1) % 2], len(PRODUCTS) * 2 * 16 * ((b - 1) // 2 + 1))
                then(eng.tensor_tensor(buf, kept[:, b * S:(b + 1) * S], fold_sb[:, side, :], ALU.mult))
                then(eng.tensor_copy(parts[:, side, 0, :], buf), parts_ready)
                then(eng.tensor_tensor(buf, buf, parts[:, side, 0, :], ALU.subtract))
                then(eng.tensor_copy(parts[:, side, 1, :], buf), parts_ready)
                then(eng.tensor_tensor(parts[:, side, 2, :], buf, parts[:, side, 1, :],
                                       ALU.subtract), parts_ready)

        block = ctx.enter_context(nc.Block())

        @block.gpsimd
        def _(pool):
            steps = [0]

            def then(ins, signal=None):
                if signal is None:
                    steps[0] += 1
                    ins.then_inc(pool_step, 1)
                    pool.wait_ge(pool_step, steps[0])
                else:
                    ins.then_inc(signal, 1)
                    done[0] += 1
                    pool.wait_ge(signal, done[0])

            done = [2 * PARTS]
            nc.gpsimd.memset(stacked[:], 0.0).then_inc(zeroed, 1)
            nc.gpsimd.memset(v_sb[:, :, :, HD:VW], 1.0).then_inc(v_ones, 1)
            pool.wait_ge(parts_ready, 2 * PARTS)
            split(nc.gpsimd, pool, then, 1, (0, 1))
            pool.wait_ge(flag_ready, 1)
            fast = pool.value_load(flag[0:1, 0:1], min_val=0, max_val=1)
            with pool.If(fast == 1):
                for b in range(2, B):
                    split(nc.gpsimd, pool, then, b, (0, 1))

        @block.sync
        def _(sp):
            for b in range(B):
                sp.dma_start(x_sb[:, b * QT:(b + 1) * QT, :],
                             x[b].rearrange("(t p) d -> p t d", p=P)).then_inc(x_in[b], 16)
            for dst, src in ((ident[:], identity), (wk_sb[:], wk), (wv_sb[:], wv), (wq_sb[:], wq),
                             (wdown_sb[:], w_down), (wup_sb[:, 0, :], w_up_k), (wup_sb[:, 1, :], w_up_v),
                             (wr_sb[:], w_router), (wo_sb[:], wo),
                             (b1_sb[:], b1.rearrange("e (c p) -> (e c) p", p=P)), (b2_sb[:], b2),
                             (rows_sb[0:1, 0:EXPERTS], b_router.rearrange("(a n) -> a n", a=1)),
                             (rows_sb[0:1, EXPERTS:EXPERTS + D], ln_w.rearrange("(a n) -> a n", a=1)),
                             (rows_sb[0:1, EXPERTS + D:], ln_b.rearrange("(a n) -> a n", a=1)), (ones_f[:], head_ones)):
                sp.dma_start(dst, src).then_inc(small_in, 16)
            sp.dma_start(fold_sb[:], fold).then_inc(const_in, 16)
            for half in range(2):
                sp.dma_start(mend_sb[half][:], mend[2 * half * P:(2 * half + 2) * P, 0:(2 * half + 2) * P]
                             .rearrange("(t p) q -> p t q", p=P)).then_inc(const_in, 16)
            sp.dma_start(w1_sb, w1.rearrange("e (c p) h -> p (e c) h", p=P)).then_inc(w1_in, 16)
            sp.dma_start(w2_sb.rearrange("p (e c) f -> p e (c f)", c=FC),
                         w2.rearrange("e h f -> h e f")).then_inc(w2_in, 16)
            sp.wait_ge(zeroed, 1)

            def stack_rows(b):
                for side in range(2):
                    for part in range(PARTS):
                        sp.wait_ge(parts_ready, (b * 2 + side) * PARTS + part + 1)
                        for n, product in enumerate(PRODUCTS):
                            if product[side] == part:
                                sp.dma_start(stacked[n * HD:(n + 1) * HD, side, b % 2, :, :],
                                             parts[:, side, part, :]).then_inc(rows_in[b % 2], 16)

            stack_rows(0)
            stack_rows(1)
            sp.wait_ge(flag_ready, 1)
            fast = sp.value_load(flag[0:1, 0:1], min_val=0, max_val=1)
            for b in range(2):
                sp.wait_ge(rows_in[b], len(PRODUCTS) * 2 * 16)
            with sp.If(fast == 1):
                for b in range(2, B):
                    sp.wait_ge(fast_scores, (b - 1) * UNITS // B)
                    stack_rows(b)
            with sp.Else():
                sp.wait_ge(qk_ready, 2 * B)
                sp.dma_start(decay_sb, decay.rearrange("(t p) k -> p t k", p=P)).then_inc(decay_in, 16)
                for sc, src in ((q_scr, qT_sb), (k_scr, kT_sb)):
                    for b in range(B):
                        sp.dma_start(sc[b * HEADS:(b + 1) * HEADS].rearrange("h d s -> d h s"),
                                     head_rows(src, b)).then_inc(scratch_out, 16)
                sp.wait_ge(scratch_out, 2 * B * 16)

                def load_head(pair, u):
                    sp.dma_start(q_head[:, u:u + 1, :], q_scr[bass.ds(pair, 1)].rearrange("a d s -> d a s")).then_inc(head_in[u], 16)
                    sp.dma_start(k_head[:, u:u + 1, :], k_scr[bass.ds(pair, 1)].rearrange("a d s -> d a s")).then_inc(head_in[u], 16)

                for u in range(SLOTS):
                    load_head(u, u)
                with sp.Fori(0, PAIRS // SLOTS - 1) as m:
                    n = m * SLOTS
                    for u in range(SLOTS):
                        sp.wait_ge(scores_ready, (n + (u + 1)) * QT)
                        load_head(n + (SLOTS + u), u)
            sp.wait_ge(cwT_psum, 1)
            for b in range(B):
                sp.dma_start(x_again[:, b * QT:(b + 1) * QT, :], x[b].rearrange("(t p) d -> p t d", p=P)).then_inc(x_back, 16)
            for t in range(TILES):
                sp.wait_ge(out_ready, t + 1)
                sp.dma_start(out[t // QT, (t % QT) * P:(t % QT + 1) * P, :], z[:, t, :]).then_inc(stored, 16)
            sp.wait_ge(stored, TILES * 16)

        @block.tensor
        def _(pe):
            pe.wait_ge(small_in, 15 * 16)
            pe.wait_ge(ones_set, 1)
            nc.tensor.transpose(ps[:, 0, 0:EXPERTS], wr_sb[:], ident[0:EXPERTS, 0:EXPERTS])
            nc.tensor.transpose(ps[:, 0, 8:40], b1_sb[:], ident[0:32, 0:32]).then_inc(prep_psum, 1)
            nc.tensor.matmul(ps[:, 1, 0:EXPERTS + 2 * D], ones_row[:], rows_sb[:], start=True, stop=True).then_inc(prep_psum, 1)
            pe.wait_ge(kv_sum, 1)
            nc.tensor.transpose(ps[:, 2, 0:D], wk_sb[:], ident[:]).then_inc(prep_psum, 1)
            pe.wait_ge(prep_copied, 3)
            nc.tensor.matmul(ps[0:LATENT, 3, 0:D], wdown_sb[:], wkvT_sb[:], start=True, stop=True).then_inc(prep_psum, 1)
            pe.wait_ge(prep_copied, 4)
            nc.tensor.matmul(ps[:, 5, 0:2 * D], wlatT_sb[:], wup_sb[:].rearrange("l a d -> l (a d)"),
                             start=True, stop=True).then_inc(prep_psum, 1)
            pe.wait_ge(prep_copied, 5)
            for b in range(B):
                pe.wait_ge(xn_ready, (b + 1) * QT)
                for t in range(QT):
                    last = nc.tensor.transpose(ps[:, b, t * P:(t + 1) * P], xn[:, b * QT + t, :], ident[:])
                last.then_inc(xnT_psum, 1)
            def norms(b):
                pe.wait_ge(squares_ready, 2 * (b + 1))
                if b:
                    pe.wait_ge(norms_read, b)
                for side in range(2):
                    last = nc.tensor.matmul(ps[0:HEADS, side, :], ones_b[:], squares[:, side, :], start=True, stop=True)
                last.then_inc(norms_psum, 1)

            for b in range(B):
                tok = slice(b * S, (b + 1) * S)
                pe.wait_ge(xnT_ready, b + 1)
                if b:
                    pe.wait_ge(qk_ready, 2 * b)
                    pe.wait_ge(v_ready, b)
                    pe.wait_ge(logits_ready, b)
                nc.tensor.matmul(ps[:, 4, :], wq_cols[:], xnT[:, tok], start=True, stop=True)
                nc.tensor.matmul(ps[:, 5, :], wrec_sb[:, 0, :], xnT[:, tok], start=True, stop=True)
                for t in range(QT):
                    tile = xnT[:, (b * QT + t) * P:(b * QT + t + 1) * P]
                    nc.tensor.matmul(ps[:, 6, t * D:(t + 1) * D], tile, wrec_sb[:, 1, :], start=True, stop=True)
                for t in range(QT):
                    tile = xnT[:, (b * QT + t) * P:(b * QT + t + 1) * P]
                    last = nc.tensor.matmul(ps[:, 7, t * EXPERTS:(t + 1) * EXPERTS], tile, wrT_sb[:], start=True, stop=True)
                last.then_inc(proj_psum, 1)
                if b:
                    norms(b - 1)
            norms(B - 1)
            pe.wait_ge(checks_ready, 1)
            nc.tensor.transpose(ps[0:1, 2, 0:P], all_finite[:], ident[:])
            nc.tensor.transpose(ps[0:1, 2, P:P + HEADS], bound_max[:], ident[0:HEADS, 0:HEADS]).then_inc(checks_psum, 1)
            for g in range(w_groups):
                src, loaded = (w1_sb, w1_in) if g < EXPERTS else (w2_sb, w2_in)
                pe.wait_ge(loaded, 16)
                if g == 0:
                    pe.wait_ge(norms_read, B)
                    pe.wait_ge(flag_ready, 1)
                if g >= 4:
                    pe.wait_ge(wT_ready, g - 3)
                for c in range(FC):
                    last = nc.tensor.transpose(ps[:, g % 4, c * P:(c + 1) * P],
                                               src[:, (g % EXPERTS) * FC + c, :], ident[:])
                last.then_inc(wT_psum, 1)
            pe.wait_ge(wT_ready, w_groups)
            pe.wait_ge(qk_ready, 2 * B)
            pe.wait_ge(v_ready, B)

            fast = pe.value_load(flag[0:1, 0:1], min_val=0, max_val=1)
            with pe.If(fast == 1):
                def scores(n):
                    group, half, g = n // (2 * GROUP), n // GROUP % 2, n % GROUP
                    b, h = divmod(group * GROUP + g, HEADS)
                    if n % (UNITS // B) == 0:
                        pe.wait_ge(rows_in[b % 2], (b // 2 + 1) * len(PRODUCTS) * 2 * 16)
                    if n >= 2:
                        pe.wait_ge(fast_probs, n - 1)
                    for k in range(2):
                        keys = (2 * half + k) * P
                        last = nc.tensor.matmul(ps[:, 2 * (n % 2) + k, :], k_rows[:, b % 2, h, keys:keys + P],
                                                q_rows[:, b % 2, h, :], start=True, stop=True)
                    last.then_inc(fast_scores, 1)

                def outputs(quad, k):
                    group, half = divmod(quad, 2)
                    tile = 2 * half + k
                    if k == 0:
                        pe.wait_ge(fast_probs, (quad + 1) * GROUP)
                    if tile == 0 and group:
                        pe.wait_ge(fast_heads, group)
                    for g in range(GROUP):
                        b, h = divmod(group * GROUP + g, HEADS)
                        last = nc.tensor.matmul(ps[32 * g:32 * g + VW, 4, :], v_sb[:, b * QT + tile, h, :],
                                                probs_fast[:, quad % 2, g, k * S:(k + 1) * S],
                                                start=(tile == 0), stop=(tile == QT - 1))
                    if k == 1:
                        last.then_inc(fast_used, 1)

                def turn(group):
                    pe.wait_ge(fast_heads, group + 1)
                    if group:
                        pe.wait_ge(fast_done, group)
                    for t in range(QT):
                        last = nc.tensor.transpose(ps[:, 5, t * P:(t + 1) * P], out_heads[:, t * P:(t + 1) * P], ident[:])
                    last.then_inc(fast_outT, 1)

                pe.wait_ge(v_ones, 1)
                scores(0)
                scores(1)
                for n in range(2, UNITS + 4):
                    if n < UNITS:
                        scores(n)
                    quad, at = divmod(n - 1 - GROUP, GROUP)
                    if 0 <= quad < QUADS and at < 2:
                        outputs(quad, at)
                    if quad >= 1 and quad % 2 == 0 and at == 2:
                        turn(quad // 2 - 1)
                turn(GROUPS - 1)
                pe.wait_ge(fast_done, GROUPS)
            with pe.Else():
                def scores(pair, u, t):
                    s = t % SLOTS
                    nc.tensor.matmul(ps[:, s, :], q_head[:, u, t * P:(t + 1) * P], k_head[:, u, :],
                                     start=True, stop=True).then_inc(scores_ready, 1)

                def transposes(s):
                    for k in range(QT):
                        last = nc.tensor.transpose(ps[:, 2 + s, k * P:(k + 1) * P], probs[:, s, k * P:(k + 1) * P], ident[:])
                    last.then_inc(probsT_psum, 1)

                def outputs(b, h, s):
                    for k in range(QT):
                        last = nc.tensor.matmul(ps[:, 4 + s, 0:HD], probsT[:, s, k * P:(k + 1) * P],
                                                v_sb[:, bass.ds(b * QT + k, 1), bass.ds(h, 1), 0:HD], start=(k == 0), stop=(k == QT - 1))
                    last.then_inc(attn_psum, 1)

                with pe.Fori(0, B) as b, pe.Fori(0, HEADS // SLOTS) as m:
                    n = b * HEADS + m * SLOTS
                    for u in range(SLOTS):
                        pe.wait_ge(head_in[u], (n * 16 + 32))
                        for t in range(QT):
                            s = t % SLOTS
                            step = (n + u) * QT + t
                            scores(n + u, u, t)
                            pe.wait_ge(probs_ready, step + 1)
                            transposes(s)
                            pe.wait_ge(probsT_ready, step + 1)
                            outputs(b, m * SLOTS + u, s)
                pe.wait_ge(attn_read, PAIRS * QT)
            pe.wait_ge(cw_ready, 1)
            for g in range(4):
                for t in range(4):
                    last = nc.tensor.transpose(ps[0:EXPERTS, g, t * P:(t + 1) * P], cw[:, g * 4 + t, :], ident[:])
            last.then_inc(cwT_psum, 1)
            pe.wait_ge(cwT_ready, 1)
            for g in range(4):
                for t in range(4):
                    last = nc.tensor.matmul(ps[:, g, t * D:(t + 1) * D], cwT[:, g * 4 + t, :], b2_sb[:], start=True, stop=True)
            last.then_inc(bias_psum, 1)
            pe.wait_ge(acc_ready, 1)

            with pe.Fori(0, B) as b:
                for e in range(EXPERTS):
                    for c in range(FC):
                        if e:
                            pe.wait_ge(hidden_ready, b * (EXPERTS * FC) + ((e - 1) * FC + c + 1))
                        nc.tensor.matmul(ps[:, c, :], w1T[:, e * FC + c, :], xnT[:, bass.ds(b * S, S)],
                                         start=True, stop=True).then_inc(hidden_psum, 1)
                    pe.wait_ge(hidden_ready, b * (EXPERTS * FC) + (e + 1) * FC)
                    if e:
                        pe.wait_ge(y_read, b * EXPERTS + e)
                    for c in range(FC):
                        for t in range(QT):
                            last = nc.tensor.matmul(ps[:, 4 + e % 2, t * D:(t + 1) * D],
                                                    hidden[:, e % 2, c, t * P:(t + 1) * P], w2T[:, e * FC + c, :],
                                                    start=(c == 0 and t == 0), stop=(c == FC - 1 and t == QT - 1),
                                                    skip_group_check=True)
                    last.then_inc(y_psum, 1)
            for b in range(B):
                for t in range(QT):
                    last = nc.tensor.transpose(ps[:, b, t * P:(t + 1) * P],
                                               attn[:, b * QT + t, :, :].rearrange("p h d -> p (h d)"), ident[:])
                last.then_inc(attnT_psum, 1)
            pe.wait_ge(y_read, B * EXPERTS)
            for b in range(B):
                pe.wait_ge(attnT_ready, b + 1)
                for t in range(QT):
                    last = nc.tensor.matmul(ps[:, 4 + b, t * D:(t + 1) * D], attnT[:, b * QT + t, :], wo_sb[:],
                                            start=True, stop=True)
                last.then_inc(wo_psum, 1)

        @block.scalar
        def _(act):
            act.wait_ge(var_ready, 1)
            nc.scalar.activation(std[:], newton[:, 0, :], ACT.Sqrt).then_inc(std_ready, 1)
            for b in range(B):
                act.wait_ge(xnT_psum, b + 1)
                nc.scalar.copy(xnT[:, b * S:(b + 1) * S], ps[:, b, :]).then_inc(xnT_ready, 1)
            for b in range(B):
                tok = slice(b * S, (b + 1) * S)
                act.wait_ge(proj_psum, b + 1)
                if b:
                    act.wait_ge(norms_psum, b)
                for side, (kept, scale) in enumerate(((qT_sb, SCALE), (kT_sb, 1.0))):
                    nc.scalar.activation(squares[:, side, :], ps[:, 4 + side, :], ACT.Square, scale=scale,
                                         accum_out=square_sums[:, 2 * b + side:2 * b + side + 1]).then_inc(squares_ready, 1)
                    nc.scalar.mul(kept[:, tok], ps[:, 4 + side, :], scale).then_inc(qk_ready, 1)
            for g in range(0, w_groups):
                dst = w1T if g < EXPERTS else w2T
                act.wait_ge(wT_psum, g + 1)
                nc.scalar.copy(dst[:, (g % EXPERTS) * FC:(g % EXPERTS + 1) * FC, :],
                               ps[:, g % 4, :].rearrange("p (c f) -> p c f", c=FC)).then_inc(wT_ready, 1)
            act.wait_ge(gap_ready, 1)
            nc.scalar.activation(top[:, 5, :], top[:, 4, :], ACT.Exp).then_inc(gap_exp, 1)
            act.wait_ge(flag_ready, 1)
            fast = act.value_load(flag[0:1, 0:1], min_val=0, max_val=1)
            with act.If(fast == 1):
                for n in range(UNITS):
                    quad, g = divmod(n, GROUP)
                    act.wait_ge(fast_fixed, n + 1)
                    if quad >= 2 and g == 0:
                        act.wait_ge(fast_used, quad - 1)
                    nc.scalar.activation(probs_fast[:, quad % 2, g, :].rearrange("p (k q) -> p k q", k=2),
                                         ps[:, 2 * (n % 2):2 * (n % 2) + 2, :], ACT.Exp).then_inc(fast_probs, 1)
            with act.Else():
                with act.Fori(0, PAIRS) as n:
                    for t in range(QT):
                        s = t % SLOTS
                        step = n * QT + t
                        act.wait_ge(max_ready, step + 1)
                        nc.scalar.activation(probs[:, s, :], decayed[:, s, :], ACT.Exp, bias=neg_max[:, s:s + 1],
                                             accum_out=row_sum[:, s:s + 1]).then_inc(probs_ready, 1)
                        act.wait_ge(probsT_psum, step + 1)
                        nc.scalar.copy(probsT[:, s, :], ps[:, 2 + s, :]).then_inc(probsT_ready, 1)
            with act.Fori(0, B) as b:
                for e in range(EXPERTS):
                    if e >= 2:
                        act.wait_ge(y_psum, b * EXPERTS + (e - 1))
                    for c in range(FC):
                        act.wait_ge(hidden_psum, b * (EXPERTS * FC) + (e * FC + c + 1))
                        nc.scalar.activation(hidden[:, e % 2, c, :], ps[:, c, :], ACT.Gelu,
                                             bias=b1T_sb[:, e * FC + c:e * FC + c + 1]).then_inc(hidden_ready, 1)
            for b in range(B):
                act.wait_ge(attnT_psum, b + 1)
                nc.scalar.copy(attnT[:, b * QT:(b + 1) * QT, :], ps[:, b, :].rearrange("p (t f) -> p t f", t=QT)).then_inc(attnT_ready, 1)
            act.wait_ge(z_var, 1)
            nc.scalar.activation(std[:], newton[:, 0, :], ACT.Sqrt).then_inc(z_std, 1)

        @block.vector
        def _(v):
            steps = [0]

            split_done = [0]

            def then(ins, signal=None):
                if signal is None:
                    steps[0] += 1
                    ins.then_inc(dve, 1)
                    v.wait_ge(dve, steps[0])
                else:
                    ins.then_inc(signal, 1)
                    split_done[0] += 1
                    v.wait_ge(signal, split_done[0])

            def refine_rstd(var, eps, waits, signal, done):
                then(nc.vector.tensor_scalar(newton[:, 0, :], var, eps, None, ALU.add))
                nc.vector.tensor_copy(newton[:, 1, :], newton[:, 0, :]).then_inc(signal, 1)
                v.wait_ge(done, 1)
                then(nc.vector.reciprocal(rstd[:], std[:]))
                then(nc.vector.tensor_tensor(newton[:, 2, :], rstd[:], rstd[:], ALU.mult))
                then(nc.vector.tensor_tensor(newton[:, 2, :], newton[:, 2, :], newton[:, 0, :], ALU.mult))
                then(nc.vector.tensor_scalar(newton[:, 2, :], newton[:, 2, :], -0.5, 1.5, ALU.mult, ALU.add))
                then(nc.vector.tensor_tensor(rstd[:], rstd[:], newton[:, 2, :], ALU.mult))

            nc.vector.memset(ones_row[:], 1.0).then_inc(ones_set, 1)
            then(nc.vector.memset(ps[:, 4, :], 0.0))
            for e in range(EXPERTS):
                last = nc.vector.memset(rank[:, :, e:e + 1], float(EXPERTS - e))
            then(last)
            for b in range(B):
                v.wait_ge(x_in[b], 16)
                for t in range(b * QT, (b + 1) * QT):
                    last = nc.vector.bn_stats(stats[:, t, :], x_sb[:, t, :])
            then(last)
            for t in range(TILES):
                last = nc.vector.bn_aggr(mv[:, t, :], stats[:, t, :])
            then(last)
            refine_rstd(mv[:, :, 1], 1e-5, None, var_ready, std_ready)
            for t in range(TILES):
                nc.vector.tensor_scalar(xn[:, t, :], x_sb[:, t, :], mv[:, t, 0:1], rstd[:, t:t + 1],
                                        ALU.subtract, ALU.mult).then_inc(xn_ready, 1)
            v.wait_ge(small_in, 15 * 16)
            nc.vector.tensor_tensor(wk_sb[:], wk_sb[:], wv_sb[:], ALU.add).then_inc(kv_sum, 1)
            then(nc.vector.tensor_copy(wq_cols[:].rearrange("p (d h) -> p d h", h=HEADS),
                                       wq_sb[:].rearrange("p (h d) -> p d h", d=HD)))
            then(nc.vector.tensor_copy(ones_b[:], ones_f[:]))
            v.wait_ge(prep_psum, 1)
            nc.vector.tensor_copy(wrT_sb[:], ps[:, 0, 0:EXPERTS])
            nc.vector.tensor_copy(b1T_sb[:], ps[:, 0, 8:40]).then_inc(prep_copied, 1)
            v.wait_ge(prep_psum, 2)
            nc.vector.tensor_copy(rows_bc[:], ps[:, 1, 0:EXPERTS + 2 * D]).then_inc(prep_copied, 1)
            v.wait_ge(prep_psum, 3)
            nc.vector.tensor_copy(wkvT_sb[:], ps[:, 2, 0:D]).then_inc(prep_copied, 1)
            v.wait_ge(prep_psum, 4)
            nc.vector.tensor_copy(wlatT_sb[:], ps[0:LATENT, 3, 0:D]).then_inc(prep_copied, 1)
            v.wait_ge(prep_psum, 5)
            then(nc.vector.tensor_copy(wrec_sb[:, 0, :].rearrange("p (d h) -> p d h", h=HEADS),
                                       ps[:, 5, 0:D].rearrange("p (h d) -> p d h", d=HD)))
            nc.vector.tensor_copy(wrec_sb[:, 1, :], ps[:, 5, D:2 * D]).then_inc(prep_copied, 1)
            def norm_maxima(b):
                v.wait_ge(norms_psum, b + 1)
                nc.vector.tensor_reduce(norm_max[:, b, :], ps[0:HEADS, 0:2, :], AX.X, ALU.max).then_inc(norms_read, 1)

            def check_range():
                v.wait_ge(squares_ready, 2 * B)
                then(nc.vector.tensor_scalar(finite[:], square_sums[:], 1e30, None, ALU.is_le))
                v.wait_ge(norms_read, B)
                then(nc.vector.tensor_reduce(all_finite[:], finite[:], AX.X, ALU.min))
                then(nc.vector.tensor_tensor(bound[:], norm_max[:, :, 0], norm_max[:, :, 1], ALU.mult))
                nc.vector.tensor_reduce(bound_max[:], bound[:], AX.X, ALU.max).then_inc(checks_ready, 1)
                v.wait_ge(checks_psum, 1)
                then(nc.vector.tensor_reduce(verdict[:, 0:1], ps[0:1, 2, 0:P], AX.X, ALU.min))
                then(nc.vector.tensor_reduce(verdict[:, 1:2], ps[0:1, 2, P:P + HEADS], AX.X, ALU.max))
                then(nc.vector.tensor_scalar(verdict[:, 2:3], verdict[:, 1:2], SAFE * SAFE, None, ALU.is_le))
                nc.vector.tensor_tensor(flag[:], verdict[:, 2:3], verdict[:, 0:1], ALU.mult).then_inc(flag_ready, 1)

            for b in range(B):
                v.wait_ge(proj_psum, b + 1)
                nc.vector.tensor_copy(v_sb[:, b * QT:(b + 1) * QT, :, 0:HD],
                                      ps[:, 6, :].rearrange("p (k h d) -> p k h d", k=QT, h=HEADS)).then_inc(v_ready, 1)
                nc.vector.tensor_tensor(logits[:, b * QT:(b + 1) * QT, :],
                                        ps[:, 7, 0:QT * EXPERTS].rearrange("p (t e) -> p t e", t=QT),
                                        rows_bc[:, None, 0:EXPERTS].to_broadcast([P, QT, EXPERTS]), ALU.add).then_inc(logits_ready, 1)
                if b:
                    norm_maxima(b - 1)
                if b == 0:
                    split(nc.vector, v, then, 0, (0, 1))
            norm_maxima(B - 1)
            check_range()
            v.wait_ge(logits_ready, B)

            def top_one(values, largest, onehot):
                ranks = top[:, 2, :]
                then(nc.vector.tensor_reduce(largest, values, AX.X, ALU.max))
                then(nc.vector.tensor_tensor(pick[:], values, largest.unsqueeze(2).to_broadcast([P, TILES, EXPERTS]), ALU.is_equal))
                then(nc.vector.tensor_tensor(pick[:], pick[:], rank[:], ALU.mult))
                then(nc.vector.tensor_reduce(ranks, pick[:], AX.X, ALU.max))
                then(nc.vector.tensor_tensor(onehot, rank[:], ranks.unsqueeze(2).to_broadcast([P, TILES, EXPERTS]), ALU.is_equal))

            top_one(logits[:], top[:, 0, :], first[:])
            then(nc.vector.scalar_tensor_tensor(logits[:], first[:], -3.0e38, logits[:], ALU.mult, ALU.add))
            top_one(logits[:], top[:, 1, :], second[:])
            nc.vector.tensor_tensor(top[:, 4, :], top[:, 1, :], top[:, 0, :], ALU.subtract).then_inc(gap_ready, 1)
            v.wait_ge(gap_exp, 1)
            then(nc.vector.tensor_scalar(top[:, 6, :], top[:, 5, :], 1.0, None, ALU.add))
            then(nc.vector.reciprocal(top[:, 6, :], top[:, 6, :]))
            then(nc.vector.tensor_tensor(top[:, 7, :], top[:, 5, :], top[:, 6, :], ALU.mult))
            then(nc.vector.tensor_tensor(first[:], first[:], top[:, 6, :].unsqueeze(2).to_broadcast([P, TILES, EXPERTS]), ALU.mult))
            then(nc.vector.tensor_tensor(second[:], second[:], top[:, 7, :].unsqueeze(2).to_broadcast([P, TILES, EXPERTS]), ALU.mult))
            nc.vector.tensor_tensor(cw[:], first[:], second[:], ALU.add).then_inc(cw_ready, 1)

            v.wait_ge(flag_ready, 1)
            fast = v.value_load(flag[0:1, 0:1], min_val=0, max_val=1)
            with v.If(fast == 1):
                v.wait_ge(const_in, 48)

                def heads(group):
                    v.wait_ge(fast_used, 2 * (group + 1))
                    if group:
                        v.wait_ge(fast_outT, group)
                    nc.vector.tensor_copy(out_heads[:], ps[:, 4, :]).then_inc(fast_heads, 1)

                def normalise(group):
                    b, h = divmod(group * GROUP, HEADS)
                    v.wait_ge(fast_outT, group + 1)
                    if group:
                        v.wait_ge(fast_done, group)
                    turned = ps[:, 5, :].rearrange("p (t g w) -> p t g w", t=QT, g=GROUP)
                    nc.vector.reciprocal(inv_fast[:], turned[:, :, :, HD:VW]).then_inc(fast_step, 1)
                    v.wait_ge(fast_step, group + 1)
                    nc.vector.tensor_tensor(attn[:, b * QT:(b + 1) * QT, h:h + GROUP, :], turned[:, :, :, 0:HD],
                                            inv_fast[:].to_broadcast([P, QT, GROUP, HD]), ALU.mult).then_inc(fast_done, 1)

                for n in range(UNITS + 2 * GROUP):
                    if n < UNITS:
                        half = n // GROUP % 2
                        wide = (2 * half + 2) * P
                        scores = ps[:, 2 * (n % 2):2 * (n % 2) + 2, 0:wide]
                        v.wait_ge(fast_scores, n + 1)
                        nc.vector.tensor_tensor(scores, scores, mend_sb[half][:],
                                                ALU.mult).then_inc(fast_fixed, 1)
                    group, at = divmod(n - 2 * GROUP, 2 * GROUP)
                    if group >= 0 and at == 3:
                        heads(group)
                    if group >= 0 and at == 6:
                        normalise(group)
            with v.Else():
                v.wait_ge(decay_in, 16)
                base = 0
                LOOP = 3
                with v.Fori(0, B) as b, v.Fori(0, HEADS) as h:
                    n = b * HEADS + h
                    for t in range(QT):
                        s = t % SLOTS
                        step = n * QT + t
                        v.wait_ge(scores_ready, step + 1)
                        nc.vector.tensor_scalar(clipped[:, s, :], ps[:, s, :], CLAMP, -CLAMP, ALU.min, ALU.max).then_inc(scores_read, 1)
                        v.wait_ge(scores_read, step + 1)
                        nc.vector.tensor_tensor(decayed[:, s, :], clipped[:, s, :], decay_sb[:, t, :], ALU.mult).then_inc(gen_step, 1)
                        v.wait_ge(gen_step, step * LOOP + (base + 1))
                        nc.vector.tensor_reduce(row_max[:, s:s + 1], decayed[:, s, :], AX.X, ALU.max).then_inc(gen_step, 1)
                        v.wait_ge(gen_step, step * LOOP + (base + 2))
                        nc.vector.tensor_scalar(neg_max[:, s:s + 1], row_max[:, s:s + 1], -1.0, None, ALU.mult).then_inc(max_ready, 1)
                        v.wait_ge(probs_ready, step + 1)
                        nc.vector.reciprocal(inv_sum[:, s:s + 1], row_sum[:, s:s + 1]).then_inc(gen_step, 1)
                        v.wait_ge(gen_step, step * LOOP + (base + 3))
                        v.wait_ge(attn_psum, step + 1)
                        nc.vector.tensor_scalar(attn[:, bass.ds(b * QT + t, 1), bass.ds(h, 1), :], ps[:, 4 + s, 0:HD].unsqueeze(1).unsqueeze(1), inv_sum[:, s:s + 1], None,
                                                ALU.mult).then_inc(attn_read, 1)
            v.wait_ge(cwT_psum, 1)
            then(nc.vector.tensor_copy(cwT.rearrange("e t p -> e (t p)"), ps[0:EXPERTS, 0:4, :].rearrange("e g p -> e (g p)")))
            nc.vector.tensor_copy(top[:, 3, :], top[:, 2, :]).then_inc(cwT_ready, 1)
            v.wait_ge(bias_psum, 1)
            nc.vector.tensor_tensor(acc[:], ps[:, 0:4, :].rearrange("p g (t d) -> p (g t) d", t=4), xn[:], ALU.add).then_inc(acc_ready, 1)
            v.wait_ge(acc_ready, 1)
            with v.Fori(0, B) as b:
                for e in range(EXPERTS):
                    v.wait_ge(y_psum, b * EXPERTS + (e + 1))
                    if e:
                        v.wait_ge(y_read, b * EXPERTS + e)
                    for t in range(QT):
                        tile = acc[:, bass.ds(b * QT + t, 1), :]
                        last = nc.vector.scalar_tensor_tensor(
                            tile, ps[:, 4 + e % 2, t * D:(t + 1) * D], cw[:, bass.ds(b * QT + t, 1), e], tile,
                            ALU.mult, ALU.add)
                    last.then_inc(y_read, 1)
            v.wait_ge(y_read, B * EXPERTS)
            for t in range(TILES):
                last = nc.vector.bn_stats(stats[:, t, :], acc[:, t, :])
            then(last)
            for t in range(TILES):
                last = nc.vector.bn_aggr(mv[:, t, :], stats[:, t, :])
            then(last)
            refine_rstd(mv[:, :, 1], 1e-12, None, z_var, z_std)
            for t in range(TILES):
                last = nc.vector.tensor_scalar(z[:, t, :], acc[:, t, :], mv[:, t, 0:1], rstd[:, t:t + 1],
                                               ALU.subtract, ALU.mult)
            then(last)
            wide = lambda a: rows_bc[:, None, EXPERTS + a * D:EXPERTS + (a + 1) * D].to_broadcast([P, TILES, D])
            then(nc.vector.tensor_tensor(z, z, wide(0), ALU.mult))
            then(nc.vector.tensor_tensor(z, z, wide(1), ALU.add))
            v.wait_ge(x_back, B * 16)
            then(nc.vector.tensor_tensor(z, z, x_again, ALU.add))
            v.wait_ge(wo_psum, B)
            for t in range(TILES):
                nc.vector.tensor_tensor(z[:, t, :], ps[:, 4 + t // QT, (t % QT) * D:(t % QT + 1) * D], z[:, t, :],
                                        ALU.add).then_inc(out_ready, 1)


NAMES = ["L0_attn_x", "L0_attn_Wq", "L0_attn_Wk", "L0_attn_Wv", "L0_attn_Wo", "L0_attn_W_down_kv",
         "L0_attn_W_up_k", "L0_attn_W_up_v", "L0_ffn_Wr", "L0_ffn_br", "L0_ffn_W1", "L0_ffn_b1",
         "L0_ffn_W2", "L0_ffn_b2", "L0_ffn_ln_w", "L0_ffn_ln_b"]


def kernel(**inputs):
    import numpy as np
    import concourse.bacc as bacc
    from concourse.bass_utils import run_bass_kernel_spmd

    nc = bacc.Bacc("TRN2", target_bir_lowering=False, num_devices=1)
    arrays = {name: np.ascontiguousarray(inputs[name]) for name in NAMES}
    at = np.arange(S, dtype=np.float32)
    arrays["decay"] = np.exp(np.float32(-0.01 * 0.01) * np.abs(at[:, None] - at[None, :])).astype(np.float32)
    rate = 0.01 * 0.01
    place = np.arange(S, dtype=np.float64)
    arrays["fold"] = np.ascontiguousarray(np.broadcast_to(
        np.stack([np.exp(-rate * place), np.exp(rate * place)]).astype(np.float32), (P, 2, S)))
    arrays["mend"] = np.exp(-2 * rate * np.maximum(place[:, None] - place[None, :], 0)).astype(np.float32)
    arrays["head_ones"] = np.tile(np.eye(HEADS, dtype=np.float32), (HD, 1))
    arrays["identity"] = np.eye(P, dtype=np.float32)
    arrays = {n: arrays[n] for n in NAMES + ["decay", "identity", "fold", "mend", "head_ones"]}
    aps = [nc.dram_tensor(n, a.shape, mybir.dt.from_np(a.dtype), kind="ExternalInput").ap() for n, a in arrays.items()]
    out = nc.dram_tensor("out", (B, S, D), fp32, kind="ExternalOutput").ap()
    build(nc, *aps, out)
    result = run_bass_kernel_spmd(nc, [arrays], core_ids=[0])
    return result.results[0]["out"]
```

```python
import concourse.bass as bass
from concourse import mybir
from contextlib import ExitStack

fp32 = mybir.dt.float32
bf16 = mybir.dt.bfloat16
i32 = mybir.dt.int32
ALU = mybir.AluOpType
ACT = mybir.ActivationFunctionType
AX = mybir.AxisListType

P = 128
B, S, D = 4, 512, 128
HEADS, HD = 16, 8
LATENT = 32
EXPERTS, F = 8, 512
QT = S // P
TILES = B * QT
PAIRS = B * HEADS
FC = F // P
CLAMP = 10000.0
SCALE = 1.0 / (float(D) ** 0.5 + 1e-8)
SLOTS = 2
SAFE = 64.0
GROUP = 4
GROUPS = PAIRS // GROUP
UNITS = 2 * PAIRS
QUADS = UNITS // GROUP
SCORE_SLOTS = 3
OUT_BANK, TURN_BANK = 6, 7
W2_BANKS = (0, 1, 2, 4)
TURN_AFTER = 4 * 4 + 1
HALVES = ((0, 3), (1, 2))
PARTS = 3
PRODUCTS = [(0, 0), (0, 1), (1, 0), (0, 2), (2, 0), (1, 1)]
TOP = 2
WORK = 40
assert WORK >= (TOP * TILES * P + EXPERTS * (P - 1)) // P and WORK % 4 == 0
PANEL = 2 * F + D + FC
VW = HD + 1


def build(nc, x, wq, wk, wv, wo, w_down, w_up_k, w_up_v, w_router, b_router, w1, b1, w2, b2, ln_w, ln_b,
          decay, identity, fold, mend, head_ones, below, counting, out):
    with ExitStack() as ctx:
        def sb(name, shape, dt=fp32):
            return ctx.enter_context(nc.sbuf_tensor(name, shape, dt))

        def sem(name):
            return ctx.enter_context(nc.semaphore(name))

        x_sb = sb("x_sb", [P, TILES, D])
        xn = x_sb
        xnT = sb("xnT", [D, TILES * P])
        early = sb("early", [D, 4, D])
        wq_sb, wk_sb, wv_sb, wq_cols = (early[:, n, :] for n in range(4))
        y_rows = early[:].rearrange("p (a c) d -> p a c d", a=2)
        wo_sb = sb("wo_sb", [D, D])
        wdown_sb = sb("wdown_sb", [D, LATENT])
        wup_sb = sb("wup_sb", [LATENT, 2, D])
        wkvT_sb = sb("wkvT_sb", [D, D])
        wlatT_sb = sb("wlatT_sb", [LATENT, D])
        wrec_sb = sb("wrec_sb", [D, 2, D])
        wr_sb = sb("wr_sb", [EXPERTS, D])
        wrT_sb = sb("wrT_sb", [D, EXPERTS])
        rows_sb = sb("rows_sb", [1, EXPERTS + 2 * D])
        rows_bc = sb("rows_bc", [P, EXPERTS + 2 * D])
        ones_row = sb("ones_row", [1, P])
        b1_sb = sb("b1_sb", [EXPERTS * FC, P])
        w_raw = sb("w_raw", [P, 2, EXPERTS * FC, P])
        w1_sb, w2_sb = w_raw[:, 0], w_raw[:, 1]
        probs_fast = w_raw[:].rearrange("p a b c -> p (a b c)").rearrange("p (q g n) -> p q g n", q=2, g=GROUP)
        panels = sb("panels", [P, EXPERTS, PANEL])
        w1T, w2T, b2_wide, b1T = (panels[:, :, a:z] for a, z in ((0, F), (F, 2 * F), (2 * F, 2 * F + D), (2 * F + D, PANEL)))
        flat = panels[:].rearrange("p e w -> p (e w)")
        gathered = flat[:, 0:TOP * TILES * D].rearrange("p (c t d) -> p c t d", c=TOP, d=D)
        z = flat[:, TOP * TILES * D:(TOP + 1) * TILES * D].rearrange("p (t d) -> p t d", d=D)
        x_again = xnT[:].rearrange("p (t d) -> p t d", t=TILES)
        ident = sb("ident", [P, P])
        stats = sb("stats", [P, TILES, 6])
        mv = sb("mv", [P, TILES, 2])
        std = sb("std", [P, TILES])
        rstd = sb("rstd", [P, TILES])
        shift = sb("shift", [P, TILES])
        newton = sb("newton", [P, 3, TILES])
        logits = sb("logits", [P, TILES, EXPERTS])
        rank = sb("rank", [P, TILES, EXPERTS])
        chosen = sb("chosen", [P, TOP, TILES, EXPERTS])
        first, second = chosen[:, 0], chosen[:, 1]
        pick = sb("pick", [P, TILES, EXPERTS])
        top = sb("top", [P, 8, TILES])
        minus_half = top[:, 3, 0:QT]
        below_sb = sb("below_sb", [P, P])
        all_ones, below_b = sb("all_ones", [P, P], bf16), sb("below_b", [P, P], bf16)
        sel = sb("sel", [P, TILES, EXPERTS], bf16)
        counting_sb = sb("counting_sb", [P, WORK])
        ends = sb("ends", [P, 3, EXPERTS])
        out_heads = sb("out_heads", [P, S])
        running = out_heads[:, 0:2 * P].rearrange("p (a t e) -> p a t e", a=2, t=TILES)
        placed = out_heads[:, 2 * P:4 * P].rearrange("p (a t e) -> p a t e", a=TOP, t=TILES)
        owner_f = out_heads[0:1, 0:WORK * EXPERTS].rearrange("p (j e) -> p j e", j=WORK)
        slot_f = sb("slot_f", [P, TOP, TILES])
        slot_i = sb("slot_i", [P, TOP, TILES], i32)
        owner_sum = sb("owner_sum", [1, WORK])
        owner = sb("owner", [1, WORK], i32)
        zeros = sb("zeros", [P, D])
        qT_sb = sb("qT_sb", [D, TILES * P])
        kT_sb = sb("kT_sb", [D, TILES * P])
        v_sb = sb("v_sb", [P, TILES, HEADS, VW])
        attn = qT_sb[:].rearrange("p (t h d) -> p t h d", t=TILES, h=HEADS)
        fold_sb = sb("fold_sb", [P, 2, S])
        mend_sb = sb("mend_sb", [P, S])
        ones_f = sb("ones_f", [P, HEADS])
        ones_b = sb("ones_b", [P, HEADS], bf16)
        squares = sb("squares", [P, 2, S], bf16)
        x_rows = squares[:].rearrange("p a s -> p (a s)").bitcast(fp32).rearrange("p (a c d) -> p a c d", a=2, c=2)
        square_sums = sb("square_sums", [P, 2 * B])
        finite = sb("finite", [P, 2 * B])
        all_finite = sb("all_finite", [P, 1])
        norm_max = sb("norm_max", [32 + HEADS, B])
        k_norm_max = sb("k_norm_max", [HEADS, B])
        bound = sb("bound", [HEADS, B])
        bound_max = sb("bound_max", [HEADS, 1])
        verdict = sb("verdict", [1, 4])
        flag = sb("flag", [1, 1], i32)
        folded = sb("folded", [P, S])
        parts = sb("parts", [P, 2, PARTS, S], bf16)
        inv_fast = sb("inv_fast", [P, QT, GROUP, 1])
        stacked = sb("stacked", [P, 2, 2, HEADS, S], bf16)
        q_rows, k_rows = stacked[:, 0], stacked[:, 1]
        words = stacked[:].rearrange("p a b h s -> p (a b h s)").bitcast(fp32)
        spot = [0]

        def over(n, size, part=P):
            a = words[0:part, spot[0]:spot[0] + n * size].rearrange("p (n s) -> p n s", n=n)
            spot[0] += n * size
            return a

        decay_sb = over(QT, S)
        q_head, k_head = over(SLOTS, S, HD), over(SLOTS, S, HD)
        clipped, decayed, probs, probsT = (over(SLOTS, S) for _ in range(4))
        loose = w_raw[:].rearrange("p a b c -> p (a b c)")
        x_cols = loose[:, 0:2 * P].rearrange("p (a s) -> p a s", a=2)
        hidden = loose[:, 2 * P:2 * P + 2 * F].rearrange("p (a c s) -> p a c s", a=2, c=FC)
        panel = loose[:, 2 * P + 2 * F:2 * P + 2 * F + 4 * PANEL].rearrange("p (a w) -> p a w", a=4)
        row_max = sb("row_max", [P, SLOTS])
        neg_max = sb("neg_max", [P, SLOTS])
        row_sum = sb("row_sum", [P, SLOTS])
        inv_sum = sb("inv_sum", [P, SLOTS])
        acc = xn
        attnT = kT_sb[:].rearrange("p (t f) -> p t f", t=TILES)

        ps = ctx.enter_context(nc.psum_tensor("ps", [P, 8, 512], fp32))
        q_scr = nc.dram_tensor("q_scr", (PAIRS, HD, S), fp32, kind="Internal").ap()
        k_scr = nc.dram_tensor("k_scr", (PAIRS, HD, S), fp32, kind="Internal").ap()
        x_scr = nc.dram_tensor("x_scr", (WORK * P, D), fp32, kind="Internal").ap()
        y_scr = nc.dram_tensor("y_scr", (WORK * P, D), fp32, kind="Internal").ap()

        x_in = [sem(f"x_in{b}") for b in range(B)]
        chain_in, first_in, late_in, w1_in, w2_in, decay_in = (sem(n) for n in ("chain_in", "first_in", "late_in", "w1_in", "w2_in", "decay_in"))
        scratch_out, stored = sem("scratch_out"), sem("stored")
        head_in = [sem(f"head_in{u}") for u in range(SLOTS)]
        dve, gen_step = sem("dve_step"), sem("gen_step")
        ones_set, var_ready, std_ready, rstd_ready, xn_ready, xn_scaled = (
            sem(n) for n in ("ones_set", "var_ready", "std_ready", "rstd_ready", "xn_ready", "xn_scaled"))
        prep_psum, prep_copied, rows_copied = sem("prep_psum"), sem("prep_copied"), sem("rows_copied")
        xnT_psum, xnT_ready = sem("xnT_psum"), sem("xnT_ready")
        w1T_psum, w1T_ready, w2T_psum, w2T_ready = (sem(n) for n in ("w1T_psum", "w1T_ready", "w2T_psum", "w2T_ready"))
        qk_psum, v_psum, logits_psum, qk_ready, v_ready, logits_ready, ones_cast = (
            sem(n) for n in ("qk_psum", "v_psum", "logits_psum", "qk_ready", "v_ready", "logits_ready", "ones_cast"))
        gap_ready, gap_exp = sem("gap_ready"), sem("gap_exp")
        scores_ready, scores_read, max_ready, probs_ready = (
            sem(n) for n in ("scores_ready", "scores_read", "max_ready", "probs_ready"))
        probsT_psum, probsT_ready, attn_psum, attn_read = (
            sem(n) for n in ("probsT_psum", "probsT_ready", "attn_psum", "attn_read"))
        zeros_set, scr_zero, sel_ready, below_cast, prefix_psum, slots_ready, owner_ready, weights_ready, scattered = (
            sem(n) for n in ("zeros_set", "scr_zero", "sel_ready", "below_cast", "prefix_psum", "slots_ready", "owner_ready", "weights_ready", "scattered"))
        x_tile_in = [sem(f"x_tile_in{u}") for u in range(2)]
        y_out = [sem(f"y_out{u}") for u in range(2)]
        y_back = [sem(f"y_back{b}") for b in range(B)]
        xT_psum, xT_read, panel_ready, hT_psum, hidden_ready, y_psum, y_read = (
            sem(n) for n in ("xT_psum", "xT_read", "panel_ready", "hT_psum", "hidden_ready", "y_psum", "y_read"))
        combine_step, acc_ready = sem("combine_step"), sem("acc_ready")
        x_back = sem("x_back")
        const_in, zeroed, v_ones = sem("const_in"), sem("zeroed"), sem("v_ones")
        squares_ready, norms_psum, norms_read, checks_ready, checks_psum, flag_ready = (
            sem(n) for n in ("squares_ready", "norms_psum", "norms_read", "checks_ready", "checks_psum", "flag_ready"))
        parts_ready = [sem("q_parts_ready"), sem("k_parts_ready")]
        rows_in = [sem(f"rows_in{u}") for u in range(2)]
        pool_step = sem("pool_step")
        fast_scores, fast_fixed, fast_probs, fast_used, fast_out, fast_heads, fast_outT, fast_done = (
            sem(n) for n in ("fast_scores", "fast_fixed", "fast_probs", "fast_used", "fast_out", "fast_heads",
                             "fast_outT", "fast_done"))
        fast_step, after_step = sem("fast_step"), sem("after_step")
        attnT_psum, attnT_ready, wo_psum, z_var, z_root, z_scaled, xb_step, rest_step, rest_ready, out_ready = (
            sem(n) for n in ("attnT_psum", "attnT_ready", "wo_psum", "z_var", "z_root", "z_scaled",
                             "xb_step", "rest_step", "rest_ready", "out_ready"))

        STATS_AT = [UNITS // 2 + n for n in (23, 35, 47, 52)]
        SCALE_AT = [UNITS // 2 + n for n in (38, 49, 56, 61)]
        PROJECT_AFTER = [GROUPS - B + b for b in range(B)]

        def project_at(n, step):
            group, at = divmod(n - TURN_AFTER - step, 2 * GROUP)
            return PROJECT_AFTER.index(group) if at == 0 and group in PROJECT_AFTER else None

        def head_rows(ap, b):
            return ap[:, b * S:(b + 1) * S]

        def split(eng, waiter, then, b, sides, buf):
            waiter.wait_ge(const_in, 6 * 16)
            for side in sides:
                kept = (qT_sb, kT_sb)[side]
                waiter.wait_ge(qk_ready, 2 * b + side + 1)
                if b:
                    waiter.wait_ge(rows_in[(b - 1) % 2], len(PRODUCTS) * 2 * 16 * ((b - 1) // 2 + 1))
                then(eng.tensor_tensor(buf, kept[:, b * S:(b + 1) * S], fold_sb[:, side, :], ALU.mult))
                then(eng.tensor_copy(parts[:, side, 0, :], buf), parts_ready[side])
                then(eng.tensor_tensor(buf, buf, parts[:, side, 0, :], ALU.subtract))
                then(eng.tensor_copy(parts[:, side, 1, :], buf), parts_ready[side])
                then(eng.tensor_tensor(parts[:, side, 2, :], buf, parts[:, side, 1, :],
                                       ALU.subtract), parts_ready[side])

        def live(i, start=0):
            return not isinstance(i, int) or start <= i < WORK

        LAG = 3
        LOOP_FROM, LOOP_TO = 2, 9

        def expert_of(eng, i):
            return eng.value_load(owner[0:1, bass.ds(i, 1)] if not isinstance(i, int) else owner[0:1, i:i + 1],
                                  min_val=0, max_val=EXPERTS - 1)

        block = ctx.enter_context(nc.Block())

        @block.gpsimd
        def _(pool):
            steps = [0]

            def then(ins, signal=None):
                if signal is None:
                    steps[0] += 1
                    ins.then_inc(pool_step, 1)
                    pool.wait_ge(pool_step, steps[0])
                else:
                    ins.then_inc(signal, 1)
                    done[signal.name] += 1
                    pool.wait_ge(signal, done[signal.name])

            done = {parts_ready[0].name: PARTS, parts_ready[1].name: 0}
            nc.gpsimd.memset(zeros[:], 0.0).then_inc(zeros_set, 1)
            nc.gpsimd.memset(all_ones[:], 1.0).then_inc(zeros_set, 1)
            nc.gpsimd.memset(words, 0.0).then_inc(zeroed, 1)
            nc.gpsimd.memset(v_sb[:, :, :, HD:VW], 1.0).then_inc(v_ones, 1)
            pool.wait_ge(const_in, 6 * 16)
            nc.gpsimd.tensor_copy(below_b[:], below_sb[:]).then_inc(below_cast, 1)
            split(nc.gpsimd, pool, then, 0, (1,), folded[:])
            pool.wait_ge(parts_ready[0], PARTS)
            split(nc.gpsimd, pool, then, 1, (0, 1), folded[:])
            pool.wait_ge(slots_ready, 1)
            pool.wait_ge(scr_zero, 16)
            for t in range(TILES):
                for c in range(TOP):
                    nc.gpsimd.indirect_dma_start(x_scr, bass.IndirectOffsetOnAxis(ap=slot_i[:, c, t:t + 1], axis=0),
                                                 xn[:, t, :], None).then_inc(scattered, 16)
            pool.wait_ge(flag_ready, 1)
            fast = pool.value_load(flag[0:1, 0:1], min_val=0, max_val=1)
            with pool.If(fast == 1):
                for b in range(2, B):
                    split(nc.gpsimd, pool, then, b, (0, 1), folded[:])
            nc.gpsimd.memset(minus_half, -0.5).then_inc(xb_step, 1)
            pool.wait_ge(x_back, B * 16)
            batch_tiles = lambda b: slice(b * QT, (b + 1) * QT)
            wide = lambda a: rows_bc[:, None, EXPERTS + a * D:EXPERTS + (a + 1) * D].to_broadcast([P, QT, D])
            for b in range(B):
                nc.gpsimd.tensor_tensor(x_again[:, batch_tiles(b), :], x_again[:, batch_tiles(b), :], wide(1), ALU.add).then_inc(xb_step, 1)
            for u in range(2):
                pool.wait_ge(y_out[u], WORK // 4 * 16)
            pool.wait_ge(scattered, TOP * TILES * 16)
            pool.wait_ge(weights_ready, 1)

            def gather(b):
                for t in range(b * QT, (b + 1) * QT):
                    for c in range(TOP):
                        nc.gpsimd.indirect_dma_start(gathered[:, c, t, :], None, y_scr,
                                                     bass.IndirectOffsetOnAxis(ap=slot_i[:, c, t:t + 1], axis=0)).then_inc(y_back[b], 16)

            def combine(b):
                pool.wait_ge(y_back[b], TOP * QT * 16)
                tiles = batch_tiles(b)
                for c in range(TOP):
                    nc.gpsimd.tensor_tensor(gathered[:, c, tiles, :], gathered[:, c, tiles, :],
                                            top[:, 6 + c, tiles].unsqueeze(2).to_broadcast([P, QT, D]), ALU.mult).then_inc(combine_step, 1)
                pool.wait_ge(combine_step, b * (TOP + 1) + TOP)
                nc.gpsimd.tensor_tensor(gathered[:, 0, tiles, :], gathered[:, 0, tiles, :], gathered[:, 1, tiles, :],
                                        ALU.add).then_inc(combine_step, 1)
                pool.wait_ge(combine_step, b * (TOP + 1) + TOP + 1)
                nc.gpsimd.tensor_tensor(acc[:, tiles, :], acc[:, tiles, :], gathered[:, 0, tiles, :], ALU.add).then_inc(acc_ready, 1)

            def take_root(b):
                tiles = batch_tiles(b)
                pool.wait_ge(z_var, b + 1)
                nc.gpsimd.tensor_tensor(rstd[:, tiles], newton[:, 0, tiles], minus_half, ALU.pow).then_inc(z_root, 1)

            def finish_rest(b):
                tiles = batch_tiles(b)
                pool.wait_ge(z_scaled, b + 1)
                nc.gpsimd.tensor_tensor(z[:, tiles, :], z[:, tiles, :], wide(0), ALU.mult).then_inc(rest_step, 1)
                pool.wait_ge(rest_step, b + 1)
                nc.gpsimd.tensor_tensor(z[:, tiles, :], z[:, tiles, :], x_again[:, tiles, :], ALU.add).then_inc(rest_ready, 1)

            gather(0)
            for b in range(1, B):
                gather(b)
                combine(b - 1)
                if b >= 2:
                    take_root(b - 2)
            combine(B - 1)
            take_root(B - 2)
            pool.wait_ge(xb_step, B + 1)
            finish_rest(0)
            take_root(B - 1)
            for b in range(1, B):
                finish_rest(b)

        @block.sync
        def _(sp):
            for b in range(B):
                sp.dma_start(x_sb[:, b * QT:(b + 1) * QT, :],
                             x[b].rearrange("(t p) d -> p t d", p=P)).then_inc(x_in[b], 16)
            row = lambda a: a.rearrange("(a n) -> a n", a=1)
            for dst, src in ((ident[:], identity), (wk_sb, wk), (wv_sb, wv), (wdown_sb[:], w_down),
                             (wup_sb[:, 0, :], w_up_k), (wup_sb[:, 1, :], w_up_v)):
                sp.dma_start(dst, src).then_inc(chain_in, 16)
            sp.dma_start(w1_sb, w1.rearrange("e (c p) h -> p (e c) h", p=P)).then_inc(w1_in, 16)
            for dst, src in ((wq_sb, wq), (wr_sb[:], w_router),
                             (b1_sb[:], b1.rearrange("e (c p) -> (e c) p", p=P)), (rows_sb[0:1, 0:EXPERTS], row(b_router)),
                             (rows_sb[0:1, EXPERTS:EXPERTS + D], row(ln_w)), (rows_sb[0:1, EXPERTS + D:], row(ln_b))):
                sp.dma_start(dst, src).then_inc(first_in, 16)
            for dst, src in ((ones_f[:], head_ones), (fold_sb[:], fold), (mend_sb[:], mend), (below_sb[:], below),
                             (counting_sb[:], counting), (wo_sb[:], wo)):
                sp.dma_start(dst, src).then_inc(const_in, 16)
            sp.dma_start(w2_sb.rearrange("p (e c) f -> p e (c f)", c=FC),
                         w2.rearrange("e h f -> h e f")).then_inc(w2_in, 16)
            sp.dma_start(b2_wide, b2.unsqueeze(0).to_broadcast([P, EXPERTS, D])).then_inc(late_in, 16)
            sp.wait_ge(zeroed, 1)

            def stack_rows(b):
                for side in range(2):
                    for part in range(PARTS):
                        sp.wait_ge(parts_ready[side], b * PARTS + part + 1)
                        for n, product in enumerate(PRODUCTS):
                            if product[side] == part:
                                sp.dma_start(stacked[n * HD:(n + 1) * HD, side, b % 2, :, :],
                                             parts[:, side, part, :]).then_inc(rows_in[b % 2], 16)

            stack_rows(0)
            sp.wait_ge(zeros_set, 1)
            sp.dma_start(x_scr.rearrange("(j p) d -> p j d", p=P), zeros[:].unsqueeze(1).to_broadcast([P, WORK, D])).then_inc(scr_zero, 16)
            stack_rows(1)
            sp.wait_ge(flag_ready, 1)
            fast = sp.value_load(flag[0:1, 0:1], min_val=0, max_val=1)
            for b in range(2):
                sp.wait_ge(rows_in[b], len(PRODUCTS) * 2 * 16)
            with sp.If(fast == 1):
                for b in range(2, B):
                    sp.wait_ge(fast_scores, 2 * (b - 1) * UNITS // B)
                    stack_rows(b)
            with sp.Else():
                sp.wait_ge(qk_ready, 2 * B)
                sp.dma_start(decay_sb, decay.rearrange("(t p) k -> p t k", p=P)).then_inc(decay_in, 16)
                for sc, src in ((q_scr, qT_sb), (k_scr, kT_sb)):
                    for b in range(B):
                        sp.dma_start(sc[b * HEADS:(b + 1) * HEADS].rearrange("h d s -> d h s"),
                                     head_rows(src, b)).then_inc(scratch_out, 16)
                sp.wait_ge(scratch_out, 2 * B * 16)

                def load_head(pair, u):
                    sp.dma_start(q_head[:, u:u + 1, :], q_scr[bass.ds(pair, 1)].rearrange("a d s -> d a s")).then_inc(head_in[u], 16)
                    sp.dma_start(k_head[:, u:u + 1, :], k_scr[bass.ds(pair, 1)].rearrange("a d s -> d a s")).then_inc(head_in[u], 16)

                for u in range(SLOTS):
                    load_head(u, u)
                with sp.Fori(0, PAIRS // SLOTS - 1) as m:
                    n = m * SLOTS
                    for u in range(SLOTS):
                        sp.wait_ge(scores_ready, (n + (u + 1)) * QT)
                        load_head(n + (SLOTS + u), u)
            sp.wait_ge(v_psum, B)
            sp.wait_ge(logits_psum, 1)
            for b in range(B):
                sp.dma_start(x_again[:, b * QT:(b + 1) * QT, :], x[b].rearrange("(t p) d -> p t d", p=P)).then_inc(x_back, 16)
            for b in range(B):
                sp.wait_ge(out_ready, b + 1)
                sp.dma_start(out[b].rearrange("(t p) d -> p t d", p=P), z[:, b * QT:(b + 1) * QT, :]).then_inc(stored, 16)
            sp.wait_ge(stored, B * 16)

        @block.tensor
        def _(pe):
            pe.wait_ge(chain_in, 6 * 16)
            nc.tensor.matmul(ps[:, 0, 0:D], wk_sb, ident[:], start=True, stop=False)
            nc.tensor.matmul(ps[:, 0, 0:D], wv_sb, ident[:], start=False, stop=True).then_inc(prep_psum, 1)
            pe.wait_ge(prep_copied, 1)
            nc.tensor.matmul(ps[0:LATENT, 1, 0:D], wdown_sb[:], wkvT_sb[:], start=True, stop=True).then_inc(prep_psum, 1)
            pe.wait_ge(prep_copied, 2)
            nc.tensor.matmul(ps[:, 2, 0:2 * D], wlatT_sb[:], wup_sb[:].rearrange("l a d -> l (a d)"),
                             start=True, stop=True).then_inc(prep_psum, 1)
            def turn_w1(e):
                bank = 3 if e >= 4 else (1, 3)[e % 2]
                if e == 0:
                    pe.wait_ge(w1_in, 16)
                elif e == 1:
                    pe.wait_ge(rows_copied, 1)
                elif e < 4:
                    pe.wait_ge(w1T_ready, e - 1)
                elif e == 4:
                    pe.wait_ge(logits_ready, 1)
                else:
                    pe.wait_ge(w1T_ready, e)
                for c in range(FC):
                    last = nc.tensor.transpose(ps[:, bank, c * P:(c + 1) * P], w1_sb[:, e * FC + c, :], ident[:])
                last.then_inc(w1T_psum, 1)

            for b in range(B):
                pe.wait_ge(xn_ready, (b + 1) * QT // 2)
                pe.wait_ge(xn_scaled, (b + 1) * QT // 2)
                for t in range(QT):
                    last = nc.tensor.transpose(ps[:, 4 + b, t * P:(t + 1) * P], xn[:, b * QT + t, :], ident[:])
                last.then_inc(xnT_psum, 1)
                if b == 1:
                    pe.wait_ge(first_in, 6 * 16)
                    pe.wait_ge(ones_set, 1)
                    nc.tensor.transpose(ps[:, 3, 0:EXPERTS], wr_sb[:], ident[0:EXPERTS, 0:EXPERTS])
                    nc.tensor.transpose(ps[:, 3, 8:40], b1_sb[:], ident[0:32, 0:32])
                    nc.tensor.matmul(ps[:, 3, 40:40 + EXPERTS + 2 * D], ones_row[:], rows_sb[:], start=True, stop=True).then_inc(prep_psum, 1)
                else:
                    turn_w1(max(b - 1, 0))
            turn_w1(3)

            def project(b):
                tok, base = slice(b * S, (b + 1) * S), b % 2 * 4
                if b < 2:
                    pe.wait_ge(prep_copied, 5)
                    pe.wait_ge(w1T_ready, 3)
                    pe.wait_ge(xnT_ready, 3 if b else 1)
                else:
                    pe.wait_ge(xnT_ready, b + 1)
                    pe.wait_ge(qk_ready, 2 * (b - 1))
                    pe.wait_ge(v_ready, b - 1)
                nc.tensor.matmul(ps[:, base, :], wq_cols, xnT[:, tok], start=True, stop=True)
                nc.tensor.matmul(ps[:, base + 1, :], wrec_sb[:, 0, :], xnT[:, tok], start=True, stop=True).then_inc(qk_psum, 1)
                for t in range(QT):
                    tile = xnT[:, (b * QT + t) * P:(b * QT + t + 1) * P]
                    last = nc.tensor.matmul(ps[:, base + 2, t * D:(t + 1) * D], tile, wrec_sb[:, 1, :], start=True, stop=True)
                last.then_inc(v_psum, 1)

            def norms(b):
                pe.wait_ge(squares_ready, 2 * (b + 1))
                pe.wait_ge(ones_cast, 1)
                pe.wait_ge(xnT_ready, B)
                if b:
                    pe.wait_ge(norms_read, b)
                for side in range(2):
                    last = nc.tensor.matmul(ps[32 * side:32 * side + HEADS, 7, :], ones_b[:], squares[:, side, :],
                                            start=True, stop=True)
                last.then_inc(norms_psum, 1)

            project(0)
            pe.wait_ge(xnT_ready, B)
            pe.wait_ge(rows_copied, 1)
            pe.wait_ge(w1T_ready, 4)
            for t in range(TILES):
                last = nc.tensor.matmul(ps[:, 3, t * EXPERTS:(t + 1) * EXPERTS], xnT[:, t * P:(t + 1) * P], wrT_sb[:],
                                        start=True, stop=True)
            last.then_inc(logits_psum, 1)
            project(1)
            turn_w1(4)
            for b in range(2, B):
                norms(b - 2)
                project(b)
                turn_w1(b + 3)
            norms(B - 2)
            norms(B - 1)
            turn_w1(7)
            pe.wait_ge(sel_ready, 1)
            pe.wait_ge(zeros_set, 2)
            pe.wait_ge(const_in, 6 * 16)
            pe.wait_ge(below_cast, 1)
            pe.wait_ge(w1T_ready, EXPERTS)
            tiles = ps[:, 3, 0:(TILES + 1) * EXPERTS].rearrange("p (t e) -> p t e", e=EXPERTS)
            nc.tensor.matmul(tiles[:, 0, :], below_b[:], sel[:, 0, :], start=True, stop=True, skip_group_check=True)
            for t in range(TILES):
                last = nc.tensor.matmul(tiles[:, t + 1:, :], all_ones[:], sel[:, t:t + 1, :].to_broadcast([P, TILES - t, EXPERTS]),
                                        start=(t == 0), stop=(t == TILES - 1), skip_group_check=True)
                if t == 0:
                    nc.tensor.matmul(tiles[:, 1:TILES, :], below_b[:], sel[:, 1:, :], start=False, stop=False, skip_group_check=True)
            last.then_inc(prefix_psum, 1)

            def turn_w2(e):
                if e == 0:
                    pe.wait_ge(w2_in, 16)
                if e >= len(W2_BANKS):
                    pe.wait_ge(w2T_ready, e - len(W2_BANKS) + 1)
                for c in range(FC):
                    last = nc.tensor.transpose(ps[:, W2_BANKS[e % 4], c * P:(c + 1) * P], w2_sb[:, e * FC + c, :], ident[:])
                last.then_inc(w2T_psum, 1)

            pe.wait_ge(qk_ready, 2 * B)
            pe.wait_ge(v_ready, B)
            for e in range(4):
                turn_w2(e)
            pe.wait_ge(checks_ready, 1)
            nc.tensor.transpose(ps[0:1, 5, 0:P], all_finite[:], ident[:])
            nc.tensor.transpose(ps[0:1, 5, P:P + HEADS], bound_max[:], ident[0:HEADS, 0:HEADS]).then_inc(checks_psum, 1)
            for e in range(4, EXPERTS):
                turn_w2(e)
            pe.wait_ge(w1T_ready, EXPERTS)
            pe.wait_ge(w2T_ready, EXPERTS)
            pe.wait_ge(flag_ready, 1)
            pe.wait_ge(slots_ready, 1)
            def turn_attention(b):
                for t in range(QT):
                    last = nc.tensor.transpose(ps[:, TURN_BANK, t * P:(t + 1) * P],
                                               attn[:, b * QT + t, :, :].rearrange("p h d -> p (h d)"), ident[:])
                last.then_inc(attnT_psum, 1)

            def project_attention(b):
                pe.wait_ge(attnT_ready, b + 1)
                for t in range(QT):
                    last = nc.tensor.matmul(ps[:, TURN_BANK, t * D:(t + 1) * D], attnT[:, b * QT + t, :], wo_sb[:],
                                            start=True, stop=True)
                last.then_inc(wo_psum, 1)

            fast = pe.value_load(flag[0:1, 0:1], min_val=0, max_val=1)
            with pe.If(fast == 1):
                def scores(n):
                    group, half, g = n // (2 * GROUP), n // GROUP % 2, n % GROUP
                    b, h = divmod(group * GROUP + g, HEADS)
                    if n % (UNITS // B) == 0:
                        pe.wait_ge(rows_in[b % 2], (b // 2 + 1) * len(PRODUCTS) * 2 * 16)
                    if n >= SCORE_SLOTS:
                        pe.wait_ge(fast_probs, n - SCORE_SLOTS + 1)
                    for k in range(2):
                        keys = HALVES[half][k] * P
                        nc.tensor.matmul(ps[:, 2 * (n % SCORE_SLOTS) + k, :], k_rows[:, b % 2, h, keys:keys + P],
                                         q_rows[:, b % 2, h, :], start=True, stop=True).then_inc(fast_scores, 1)

                def outputs(quad, chunk):
                    k, side = divmod(chunk, 2)
                    queries = slice(side * S // 2, (side + 1) * S // 2)
                    group, half = divmod(quad, 2)
                    tile = HALVES[half][k]
                    first_tile, last_tile = (half, k) == (0, 0), (half, k) == (1, 1)
                    if chunk == 0:
                        pe.wait_ge(fast_probs, (quad + 1) * GROUP)
                    if first_tile and side == 0 and group:
                        pe.wait_ge(fast_heads, group)
                    for g in range(GROUP):
                        b, h = divmod(group * GROUP + g, HEADS)
                        last = nc.tensor.matmul(ps[32 * g:32 * g + VW, OUT_BANK, queries], v_sb[:, b * QT + tile, h, :],
                                                probs_fast[:, quad % 2, g, k * S + queries.start:k * S + queries.stop],
                                                start=first_tile and side == 0,
                                                stop=last_tile and side == 1, skip_group_check=True)
                    if chunk == 3:
                        last.then_inc(fast_used, 1)

                def turn(group):
                    pe.wait_ge(fast_heads, group + 1)
                    if group:
                        pe.wait_ge(fast_done, group)
                    if group - 1 in PROJECT_AFTER:
                        pe.wait_ge(out_ready, PROJECT_AFTER.index(group - 1) + 1)
                    for t in range(QT):
                        last = nc.tensor.transpose(ps[:, TURN_BANK, t * P:(t + 1) * P], out_heads[:, t * P:(t + 1) * P], ident[:])
                    last.then_inc(fast_outT, 1)

                def attend(part):
                    units, quads, groups = (range(part * m // 2, (part + 1) * m // 2) for m in (UNITS, QUADS, GROUPS))
                    for n in range(units[0], units[-1] + 1 + 5 * GROUP):
                        if n in units:
                            scores(n)
                        quad, at = divmod(n - GROUP - 2, GROUP)
                        if quad in quads:
                            for chunk in ((0,), (1, 2), (3,), ())[at]:
                                outputs(quad, chunk)
                        group, at = divmod(n - TURN_AFTER, 2 * GROUP)
                        if group in groups and at == 0:
                            turn(group)
                        if part and (b := project_at(n, 4)) is not None:
                            pe.wait_ge(fast_done, PROJECT_AFTER[b] + 1)
                            turn_attention(b)
                        if part and (b := project_at(n, 6)) is not None:
                            project_attention(b)
                    pe.wait_ge(fast_done, groups[-1] + 1)

                pe.wait_ge(v_ones, 1)
                attend(0)
            with pe.Else():
                def pair_scores(pair, u, t):
                    s = t % SLOTS
                    nc.tensor.matmul(ps[:, s, :], q_head[:, u, t * P:(t + 1) * P], k_head[:, u, :],
                                     start=True, stop=True).then_inc(scores_ready, 1)

                def transposes(s):
                    for k in range(QT):
                        last = nc.tensor.transpose(ps[:, 2 + s, k * P:(k + 1) * P], probs[:, s, k * P:(k + 1) * P], ident[:])
                    last.then_inc(probsT_psum, 1)

                def pair_outputs(b, h, s):
                    for k in range(QT):
                        last = nc.tensor.matmul(ps[:, 4 + s, 0:HD], probsT[:, s, k * P:(k + 1) * P],
                                                v_sb[:, bass.ds(b * QT + k, 1), bass.ds(h, 1), 0:HD], start=(k == 0), stop=(k == QT - 1))
                    last.then_inc(attn_psum, 1)

                with pe.Fori(0, B) as b, pe.Fori(0, HEADS // SLOTS) as m:
                    n = b * HEADS + m * SLOTS
                    for u in range(SLOTS):
                        pe.wait_ge(head_in[u], (n * 16 + 32))
                        for t in range(QT):
                            s = t % SLOTS
                            step = (n + u) * QT + t
                            pair_scores(n + u, u, t)
                            pe.wait_ge(probs_ready, step + 1)
                            transposes(s)
                            pe.wait_ge(probsT_ready, step + 1)
                            pair_outputs(b, m * SLOTS + u, s)
                pe.wait_ge(attn_read, PAIRS * QT)
            def step(q, u):
                i = 4 * q + u
                if live(i):
                    pe.wait_ge(x_tile_in[u // 2], 16 * (q + 1))
                    if live(i, 2):
                        pe.wait_ge(xT_read, i - 1)
                    nc.tensor.transpose(ps[:, 4 + u % 2, 0:P], x_rows[:, u // 2, u % 2, :], ident[:]).then_inc(xT_psum, 1)
                i = 4 * q + (u - 1)
                if live(i):
                    pe.wait_ge(xT_read, i + 1)
                    pe.wait_ge(panel_ready, i + 1)
                    if live(i, 2):
                        pe.wait_ge(hidden_ready, i - 1)
                    s = (u - 1) % 2
                    for c in range(FC):
                        last = nc.tensor.matmul(ps[:, s, c * P:(c + 1) * P], panel[:, (u - 1) % 4, c * P:(c + 1) * P],
                                                x_cols[:, s, :], start=True, stop=True)
                    last.then_inc(hT_psum, 1)
                i = 4 * q + (u - 2)
                if live(i):
                    pe.wait_ge(hidden_ready, i + 1)
                    if live(i, 1):
                        pe.wait_ge(y_read, i)
                    for c in range(FC):
                        last = nc.tensor.matmul(ps[:, 7, 0:D], hidden[:, u % 2, c, :],
                                                panel[:, (u - 2) % 4, F + c * D:F + (c + 1) * D],
                                                start=(c == 0), stop=(c == FC - 1))
                    last.then_inc(y_psum, 1)

            for n in range(4 * LOOP_FROM):
                step(n // 4, n % 4)
            with pe.Fori(0, LOOP_TO - LOOP_FROM) as m:
                for u in range(4):
                    step(m + LOOP_FROM, u)
            for n in range(4 * LOOP_TO, WORK + LAG):
                step(n // 4, n % 4)
            pe.wait_ge(y_read, WORK)
            with pe.If(fast == 1):
                attend(1)
            with pe.Else():
                for b in range(B):
                    if b:
                        pe.wait_ge(out_ready, b)
                    turn_attention(b)
                    project_attention(b)

        @block.scalar
        def _(act):
            act.wait_ge(var_ready, 1)
            nc.scalar.activation(std[:], newton[:, 0, :], ACT.Sqrt).then_inc(std_ready, 1)
            act.wait_ge(prep_psum, 1)
            nc.scalar.copy(wkvT_sb[:], ps[:, 0, 0:D]).then_inc(prep_copied, 1)
            act.wait_ge(prep_psum, 2)
            nc.scalar.copy(wlatT_sb[:], ps[0:LATENT, 1, 0:D]).then_inc(prep_copied, 1)
            act.wait_ge(prep_psum, 3)
            nc.scalar.copy(wrec_sb[:, 0, :].rearrange("p (d h) -> p d h", h=HEADS), ps[:, 2, 0:D].rearrange("p (h d) -> p d h", d=HD))
            nc.scalar.copy(wrec_sb[:, 1, :], ps[:, 2, D:2 * D]).then_inc(prep_copied, 1)

            def scale_tokens(b):
                for t in range(b * QT + 2, b * QT + QT):
                    nc.scalar.activation(xn[:, t, :], x_sb[:, t, :], ACT.Identity, scale=rstd[:, t:t + 1],
                                         bias=shift[:, t:t + 1]).then_inc(xn_scaled, 1)

            act.wait_ge(rstd_ready, 1)
            scale_tokens(0)
            for b in range(B):
                if b + 1 < B:
                    scale_tokens(b + 1)
                act.wait_ge(xnT_psum, b + 1)
                nc.scalar.copy(xnT[:, b * S:(b + 1) * S], ps[:, 4 + b, :]).then_inc(xnT_ready, 1)
                if b == 1:
                    act.wait_ge(prep_psum, 4)
                    nc.scalar.copy(wq_cols.rearrange("p (d h) -> p d h", h=HEADS), wq_sb.rearrange("p (h d) -> p d h", d=HD)).then_inc(prep_copied, 1)
                    nc.scalar.copy(wrT_sb[:], ps[:, 3, 0:EXPERTS])
                    nc.scalar.copy(b1T, ps[:, 3, 8:40].rearrange("p (e c) -> p e c", c=FC)).then_inc(prep_copied, 1)
                    nc.scalar.copy(rows_bc[:], ps[:, 3, 40:40 + EXPERTS + 2 * D]).then_inc(rows_copied, 1)
            for b in range(B):
                tok, base = slice(b * S, (b + 1) * S), b % 2 * 4
                act.wait_ge(qk_psum, b + 1)
                if b:
                    act.wait_ge(norms_psum, b)
                for side, (kept, scale) in enumerate(((qT_sb, SCALE), (kT_sb, 1.0))):
                    nc.scalar.activation(squares[:, side, :], ps[:, base + side, :], ACT.Square, scale=scale,
                                         accum_out=square_sums[:, 2 * b + side:2 * b + side + 1]).then_inc(squares_ready, 1)
                    nc.scalar.mul(kept[:, tok], ps[:, base + side, :], scale).then_inc(qk_ready, 1)
                act.wait_ge(v_psum, b + 1)
                nc.scalar.copy(v_sb[:, b * QT:(b + 1) * QT, :, 0:HD],
                               ps[:, base + 2, :].rearrange("p (k h d) -> p k h d", k=QT, h=HEADS)).then_inc(v_ready, 1)
            for e in range(EXPERTS):
                act.wait_ge(w2T_psum, e + 1)
                nc.scalar.copy(w2T[:, e, :], ps[:, W2_BANKS[e % 4], :]).then_inc(w2T_ready, 1)
            def heads(group):
                act.wait_ge(fast_used, 2 * (group + 1))
                if group:
                    act.wait_ge(fast_outT, group)
                else:
                    act.wait_ge(owner_ready, 1)
                nc.scalar.copy(out_heads[:], ps[:, OUT_BANK, :]).then_inc(fast_heads, 1)

            def copy_attention(b):
                act.wait_ge(attnT_psum, b + 1)
                nc.scalar.copy(attnT[:, b * QT:(b + 1) * QT, :],
                               ps[:, TURN_BANK, :].rearrange("p (t f) -> p t f", t=QT)).then_inc(attnT_ready, 1)

            act.wait_ge(gap_ready, 1)
            nc.scalar.activation(top[:, 5, :], top[:, 4, :], ACT.Exp).then_inc(gap_exp, 1)
            act.wait_ge(flag_ready, 1)
            fast = act.value_load(flag[0:1, 0:1], min_val=0, max_val=1)
            with act.If(fast == 1):
                def attend(part):
                    for n in range(part * UNITS // 2, (part + 1) * UNITS // 2 + 5 * GROUP):
                        group, at = divmod(n - 3 * GROUP, 2 * GROUP)
                        if at == 0 and group in range(part * GROUPS // 2, (part + 1) * GROUPS // 2):
                            heads(group)
                        if part and (b := project_at(n, 3)) is not None:
                            copy_attention(b)
                        if n >= (part + 1) * UNITS // 2:
                            continue
                        quad, g = divmod(n, GROUP)
                        act.wait_ge(fast_fixed, n + 1)
                        if quad >= 2 and g == 0:
                            act.wait_ge(fast_used, quad - 1)
                        nc.scalar.activation(probs_fast[:, quad % 2, g, :].rearrange("p (k q) -> p k q", k=2),
                                             ps[:, 2 * (n % SCORE_SLOTS):2 * (n % SCORE_SLOTS) + 2, :], ACT.Exp).then_inc(fast_probs, 1)

                attend(0)
            with act.Else():
                with act.Fori(0, PAIRS) as n:
                    for t in range(QT):
                        s = t % SLOTS
                        step = n * QT + t
                        act.wait_ge(max_ready, step + 1)
                        nc.scalar.activation(probs[:, s, :], decayed[:, s, :], ACT.Exp, bias=neg_max[:, s:s + 1],
                                             accum_out=row_sum[:, s:s + 1]).then_inc(probs_ready, 1)
                        act.wait_ge(probsT_psum, step + 1)
                        nc.scalar.copy(probsT[:, s, :], ps[:, 2 + s, :]).then_inc(probsT_ready, 1)
            act.wait_ge(scattered, TOP * TILES * 16)
            act.wait_ge(owner_ready, 1)

            def load_pair(i, slot):
                act.dma_start(x_rows[:, slot], x_scr[bass.ds(i * P, 2 * P)].rearrange("(c p) d -> p c d", p=P)).then_inc(x_tile_in[slot], 16)

            def step(q, u):
                i = 4 * q + u
                if u % 2 and live(i + 4):
                    act.wait_ge(xT_psum, i + 1)
                    load_pair(i + 3, u // 2)
                i = 4 * q + (u - 1)
                if live(i):
                    act.wait_ge(hT_psum, i + 1)
                    if live(i, 2):
                        act.wait_ge(y_psum, i - 1)
                    s, biases = (u - 1) % 2, 2 * F + D
                    for c in range(FC):
                        last = nc.scalar.activation(hidden[:, s, c, :], ps[:, s, c * P:(c + 1) * P], ACT.Gelu,
                                                    bias=panel[:, (u - 1) % 4, biases + c:biases + c + 1])
                    last.then_inc(hidden_ready, 1)
                i = 4 * q + (u - 3)
                if u % 2 == 0 and live(i):
                    act.wait_ge(y_read, i + 1)
                    act.dma_start(y_scr[bass.ds((i - 1) * P, 2 * P)].rearrange("(c p) d -> p c d", p=P),
                                  y_rows[:, u // 2]).then_inc(y_out[u // 2], 16)

            for n in range(2):
                load_pair(2 * n, n)
            for n in range(4 * LOOP_FROM):
                step(n // 4, n % 4)
            with act.Fori(0, LOOP_TO - LOOP_FROM) as m:
                for u in range(4):
                    step(m + LOOP_FROM, u)
            for n in range(4 * LOOP_TO, WORK + LAG):
                step(n // 4, n % 4)
            with act.If(fast == 1):
                attend(1)
            with act.Else():
                for b in range(B):
                    copy_attention(b)

        @block.vector
        def _(v):
            steps = [0]

            split_done = [0]

            def then(ins, signal=None):
                if signal is None:
                    steps[0] += 1
                    ins.then_inc(dve, 1)
                    v.wait_ge(dve, steps[0])
                else:
                    ins.then_inc(signal, 1)
                    split_done[0] += 1
                    v.wait_ge(signal, split_done[0])

            def token_stats(b):
                tiles = range(b * QT, (b + 1) * QT)
                v.wait_ge(acc_ready, b + 1)
                for t in tiles:
                    last = nc.vector.bn_stats(stats[:, t, :], acc[:, t, :])
                then(last)
                for t in tiles:
                    last = nc.vector.bn_aggr(mv[:, t, :], stats[:, t, :])
                then(last)
                nc.vector.tensor_scalar(newton[:, 0, tiles[0]:tiles[-1] + 1], mv[:, tiles[0]:tiles[-1] + 1, 1], 1e-12, None,
                                        ALU.add).then_inc(z_var, 1)

            def scale_tokens(b):
                tiles = slice(b * QT, (b + 1) * QT)
                v.wait_ge(z_root, b + 1)
                then(nc.vector.tensor_tensor(newton[:, 2, tiles], rstd[:, tiles], rstd[:, tiles], ALU.mult))
                then(nc.vector.tensor_tensor(newton[:, 2, tiles], newton[:, 2, tiles], newton[:, 0, tiles], ALU.mult))
                then(nc.vector.tensor_scalar(newton[:, 2, tiles], newton[:, 2, tiles], -0.5, 1.5, ALU.mult, ALU.add))
                then(nc.vector.tensor_tensor(rstd[:, tiles], rstd[:, tiles], newton[:, 2, tiles], ALU.mult))
                for t in range(b * QT, (b + 1) * QT):
                    last = nc.vector.tensor_scalar(z[:, t, :], acc[:, t, :], mv[:, t, 0:1], rstd[:, t:t + 1], ALU.subtract, ALU.mult)
                last.then_inc(z_scaled, 1)

            def add_projection(b):
                tiles = slice(b * QT, (b + 1) * QT)
                v.wait_ge(wo_psum, b + 1)
                v.wait_ge(rest_ready, b + 1)
                nc.vector.tensor_tensor(z[:, tiles, :], ps[:, TURN_BANK, :].rearrange("p (t d) -> p t d", d=D), z[:, tiles, :],
                                        ALU.add).then_inc(out_ready, 1)

            def refine_rstd(var, eps, waits, signal, done):
                then(nc.vector.tensor_scalar(newton[:, 0, :], var, eps, None, ALU.add))
                nc.vector.tensor_copy(newton[:, 1, :], newton[:, 0, :]).then_inc(signal, 1)
                v.wait_ge(done, 1)
                then(nc.vector.reciprocal(rstd[:], std[:]))
                then(nc.vector.tensor_tensor(newton[:, 2, :], rstd[:], rstd[:], ALU.mult))
                then(nc.vector.tensor_tensor(newton[:, 2, :], newton[:, 2, :], newton[:, 0, :], ALU.mult))
                then(nc.vector.tensor_scalar(newton[:, 2, :], newton[:, 2, :], -0.5, 1.5, ALU.mult, ALU.add))
                then(nc.vector.tensor_tensor(rstd[:], rstd[:], newton[:, 2, :], ALU.mult))

            nc.vector.memset(ones_row[:], 1.0).then_inc(ones_set, 1)
            for e in range(EXPERTS):
                last = nc.vector.memset(rank[:, :, e:e + 1], float(EXPERTS - e))
            then(last)
            for b in range(B):
                v.wait_ge(x_in[b], 16)
                for t in range(b * QT, (b + 1) * QT):
                    last = nc.vector.bn_stats(stats[:, t, :], x_sb[:, t, :])
            then(last)
            for t in range(TILES):
                last = nc.vector.bn_aggr(mv[:, t, :], stats[:, t, :])
            then(last)
            refine_rstd(mv[:, :, 1], 1e-5, None, var_ready, std_ready)
            nc.vector.scalar_tensor_tensor(shift[:], mv[:, :, 0], -1.0, rstd[:], ALU.mult, ALU.mult).then_inc(rstd_ready, 1)
            for b in range(B):
                for t in range(b * QT, b * QT + 2):
                    nc.vector.tensor_scalar(xn[:, t, :], x_sb[:, t, :], mv[:, t, 0:1], rstd[:, t:t + 1],
                                            ALU.subtract, ALU.mult).then_inc(xn_ready, 1)
            v.wait_ge(const_in, 6 * 16)
            nc.vector.tensor_copy(ones_b[:], ones_f[:]).then_inc(ones_cast, 1)

            def norm_maxima(b):
                v.wait_ge(norms_psum, b + 1)
                nc.vector.tensor_reduce(norm_max[:, b:b + 1], ps[0:32 + HEADS, 7, :], AX.X, ALU.max).then_inc(norms_read, 1)

            def read_w1(e):
                v.wait_ge(w1T_psum, e + 1)
                nc.vector.tensor_copy(w1T[:, e, :], ps[:, 3 if e >= 4 else (1, 3)[e % 2], :]).then_inc(w1T_ready, 1)

            for e in range(4):
                read_w1(e)
            split(nc.vector, v, then, 0, (0,), out_heads[:])
            v.wait_ge(logits_psum, 1)
            v.wait_ge(rows_copied, 1)
            nc.vector.tensor_tensor(logits[:], ps[:, 3, 0:TILES * EXPERTS].rearrange("p (t e) -> p t e", t=TILES),
                                    rows_bc[:, None, 0:EXPERTS].to_broadcast([P, TILES, EXPERTS]), ALU.add).then_inc(logits_ready, 1)
            v.wait_ge(logits_ready, 1)
            def top_one(values, largest, onehot):
                ranks = top[:, 2, :]
                then(nc.vector.tensor_reduce(largest, values, AX.X, ALU.max))
                then(nc.vector.tensor_tensor(pick[:], values, largest.unsqueeze(2).to_broadcast([P, TILES, EXPERTS]), ALU.is_equal))
                then(nc.vector.tensor_tensor(pick[:], pick[:], rank[:], ALU.mult))
                then(nc.vector.tensor_reduce(ranks, pick[:], AX.X, ALU.max))
                then(nc.vector.tensor_tensor(onehot, rank[:], ranks.unsqueeze(2).to_broadcast([P, TILES, EXPERTS]), ALU.is_equal))

            top_one(logits[:], top[:, 0, :], first)
            then(nc.vector.scalar_tensor_tensor(logits[:], first, -3.0e38, logits[:], ALU.mult, ALU.add))
            top_one(logits[:], top[:, 1, :], second)
            nc.vector.tensor_tensor(top[:, 4, :], top[:, 1, :], top[:, 0, :], ALU.subtract).then_inc(gap_ready, 1)
            nc.vector.tensor_tensor(sel[:], first, second, ALU.add).then_inc(sel_ready, 1)
            read_w1(4)
            for b in range(2):
                norm_maxima(b)
                read_w1(b + 5)
            for b in range(2, B):
                norm_maxima(b)
            read_w1(7)
            v.wait_ge(v_ready, B)
            then(nc.vector.memset(ps[:, OUT_BANK, :], 0.0))
            v.wait_ge(squares_ready, 2 * B)
            then(nc.vector.tensor_scalar(finite[:], square_sums[:], 1e30, None, ALU.is_le))
            v.wait_ge(norms_read, B)
            then(nc.vector.tensor_reduce(all_finite[:], finite[:], AX.X, ALU.min))
            then(nc.vector.tensor_copy(k_norm_max[:], norm_max[32:32 + HEADS, :]))
            then(nc.vector.tensor_tensor(bound[:], norm_max[0:HEADS, :], k_norm_max[:], ALU.mult))
            nc.vector.tensor_reduce(bound_max[:], bound[:], AX.X, ALU.max).then_inc(checks_ready, 1)
            v.wait_ge(checks_psum, 1)
            then(nc.vector.tensor_reduce(verdict[:, 0:1], ps[0:1, 5, 0:P], AX.X, ALU.min))
            then(nc.vector.tensor_reduce(verdict[:, 1:2], ps[0:1, 5, P:P + HEADS], AX.X, ALU.max))
            then(nc.vector.tensor_scalar(verdict[:, 2:3], verdict[:, 1:2], SAFE * SAFE, None, ALU.is_le))
            nc.vector.tensor_tensor(flag[:], verdict[:, 2:3], verdict[:, 0:1], ALU.mult).then_inc(flag_ready, 1)
            v.wait_ge(prefix_psum, 1)
            multiples, over_them = running[:, 0, :, 0], placed[:, 0].rearrange("p t e -> p (t e)").rearrange("p (e t) -> p e t", e=EXPERTS)
            nc.vector.tensor_copy(ends[:, 0, :], ps[:, 3, P:P + EXPERTS])
            then(nc.vector.tensor_scalar(multiples, counting_sb[:, 0:TILES], float(P), None, ALU.mult))
            then(nc.vector.tensor_tensor(over_them, multiples.unsqueeze(1).to_broadcast([P, EXPERTS, TILES]),
                                         ends[:, 0, :].unsqueeze(2).to_broadcast([P, EXPERTS, TILES]), ALU.is_lt))
            then(nc.vector.tensor_reduce(ends[:, 2, :], over_them, AX.X, ALU.add))
            then(nc.vector.tensor_copy(ends[:, 0, :], ends[:, 2, :]))
            for n, reach in enumerate((1, 2, 4)):
                old, new = ends[:, n % 2], ends[:, (n + 1) % 2]
                nc.vector.tensor_copy(new[:, 0:reach], old[:, 0:reach])
                then(nc.vector.tensor_tensor(new[:, reach:], old[:, reach:], old[:, 0:EXPERTS - reach], ALU.add))
            then(nc.vector.tensor_tensor(ends[:, 2, :], ends[:, 1, :], ends[:, 2, :], ALU.subtract))
            then(nc.vector.scalar_tensor_tensor(running[:, 1], ends[:, 2, :].unsqueeze(1).to_broadcast([P, TILES, EXPERTS]), float(P),
                                                ps[:, 3, 0:P].rearrange("p (t e) -> p t e", t=TILES), ALU.mult, ALU.add))
            then(nc.vector.tensor_tensor(placed, chosen[:], running[:, 1].unsqueeze(1).to_broadcast([P, TOP, TILES, EXPERTS]), ALU.mult))
            then(nc.vector.tensor_reduce(slot_f[:], placed, AX.X, ALU.add))
            nc.vector.tensor_copy(slot_i[:], slot_f[:]).then_inc(slots_ready, 1)
            then(nc.vector.tensor_tensor(owner_f, ends[0:1, 1, :].unsqueeze(1).to_broadcast([1, WORK, EXPERTS]),
                                         counting_sb[0:1, :].unsqueeze(2).to_broadcast([1, WORK, EXPERTS]), ALU.is_le))
            then(nc.vector.tensor_reduce(owner_sum[:], owner_f, AX.X, ALU.add))
            nc.vector.tensor_scalar(owner[:], owner_sum[:], float(EXPERTS - 1), None, ALU.min).then_inc(owner_ready, 1)

            v.wait_ge(flag_ready, 1)
            fast = v.value_load(flag[0:1, 0:1], min_val=0, max_val=1)
            with v.If(fast == 1):
                v.wait_ge(const_in, 6 * 16)

                def normalise(group):
                    b, h = divmod(group * GROUP, HEADS)
                    v.wait_ge(fast_outT, group + 1)
                    if group:
                        v.wait_ge(fast_done, group)
                    turned = ps[:, TURN_BANK, :].rearrange("p (t g w) -> p t g w", t=QT, g=GROUP)
                    nc.vector.reciprocal(inv_fast[:], turned[:, :, :, HD:VW]).then_inc(fast_step, 1)
                    v.wait_ge(fast_step, group + 1)
                    nc.vector.tensor_tensor(attn[:, b * QT:(b + 1) * QT, h:h + GROUP, :], turned[:, :, :, 0:HD],
                                            inv_fast[:].to_broadcast([P, QT, GROUP, HD]), ALU.mult).then_inc(fast_done, 1)

                def attend(part):
                    units, groups = (range(part * m // 2, (part + 1) * m // 2) for m in (UNITS, GROUPS))
                    for n in range(units[0], units[-1] + 1 + 5 * GROUP):
                        if n in units:
                            half = n // GROUP % 2
                            for k, tile in enumerate(HALVES[half]):
                                wide = (tile + 1) * P
                                v.wait_ge(fast_scores, 2 * n + k + 1)
                                scores = ps[:, 2 * (n % SCORE_SLOTS) + k, 0:wide]
                                last = nc.vector.tensor_tensor(scores, scores, mend_sb[:, S - wide:], ALU.mult)
                            last.then_inc(fast_fixed, 1)
                        group, at = divmod(n - TURN_AFTER, 2 * GROUP)
                        if group in groups and at == 2:
                            normalise(group)
                        if part and n in STATS_AT:
                            token_stats(STATS_AT.index(n))
                        if part and n in SCALE_AT:
                            scale_tokens(SCALE_AT.index(n))
                        if part and (b := project_at(n, 7)) is not None:
                            add_projection(b)

                attend(0)
            with v.Else():
                v.wait_ge(decay_in, 16)
                base = 0
                LOOP = 3
                with v.Fori(0, B) as b, v.Fori(0, HEADS) as h:
                    n = b * HEADS + h
                    for t in range(QT):
                        s = t % SLOTS
                        step = n * QT + t
                        v.wait_ge(scores_ready, step + 1)
                        nc.vector.tensor_scalar(clipped[:, s, :], ps[:, s, :], CLAMP, -CLAMP, ALU.min, ALU.max).then_inc(scores_read, 1)
                        v.wait_ge(scores_read, step + 1)
                        nc.vector.tensor_tensor(decayed[:, s, :], clipped[:, s, :], decay_sb[:, t, :], ALU.mult).then_inc(gen_step, 1)
                        v.wait_ge(gen_step, step * LOOP + (base + 1))
                        nc.vector.tensor_reduce(row_max[:, s:s + 1], decayed[:, s, :], AX.X, ALU.max).then_inc(gen_step, 1)
                        v.wait_ge(gen_step, step * LOOP + (base + 2))
                        nc.vector.tensor_scalar(neg_max[:, s:s + 1], row_max[:, s:s + 1], -1.0, None, ALU.mult).then_inc(max_ready, 1)
                        v.wait_ge(probs_ready, step + 1)
                        nc.vector.reciprocal(inv_sum[:, s:s + 1], row_sum[:, s:s + 1]).then_inc(gen_step, 1)
                        v.wait_ge(gen_step, step * LOOP + (base + 3))
                        v.wait_ge(attn_psum, step + 1)
                        nc.vector.tensor_scalar(attn[:, bass.ds(b * QT + t, 1), bass.ds(h, 1), :], ps[:, 4 + s, 0:HD].unsqueeze(1).unsqueeze(1), inv_sum[:, s:s + 1], None,
                                                ALU.mult).then_inc(attn_read, 1)
            v.wait_ge(gap_exp, 1)
            then(nc.vector.tensor_scalar(top[:, 6, :], top[:, 5, :], 1.0, None, ALU.add))
            then(nc.vector.reciprocal(top[:, 6, :], top[:, 6, :]))
            nc.vector.tensor_tensor(top[:, 7, :], top[:, 5, :], top[:, 6, :], ALU.mult).then_inc(weights_ready, 1)
            v.wait_ge(late_in, 16)
            def load_panel(q, u):
                i = 4 * q + u
                e = expert_of(v, i)
                if live(i, 4):
                    v.wait_ge(y_read, i - 3)
                nc.vector.tensor_copy(panel[:, u % 4:u % 4 + 1, :], panels[:, bass.ds(e, 1), :]).then_inc(panel_ready, 1)

            def step(q, u):
                i = 4 * q + u
                if live(i):
                    v.wait_ge(xT_psum, i + 1)
                    if live(i, 2):
                        v.wait_ge(hT_psum, i - 1)
                    nc.vector.tensor_copy(x_cols[:, u % 2, :], ps[:, 4 + u % 2, 0:P]).then_inc(xT_read, 1)
                if live(4 * q + (u + 1)):
                    load_panel(q, u + 1)
                i = 4 * q + (u - 2)
                if live(i):
                    pair, at = divmod(u - 2, 4)
                    v.wait_ge(y_psum, i + 1)
                    if at % 2 == 0 and live(i, 4):
                        v.wait_ge(y_out[at // 2], 16 * (q + pair))
                    nc.vector.tensor_tensor(y_rows[:, at // 2, at % 2, :], ps[:, 7, 0:D], panel[:, at, 2 * F:2 * F + D],
                                            ALU.add).then_inc(y_read, 1)

            load_panel(0, 0)
            for n in range(4 * LOOP_FROM):
                step(n // 4, n % 4)
            with v.Fori(0, LOOP_TO - LOOP_FROM) as m:
                for u in range(4):
                    step(m + LOOP_FROM, u)
            for n in range(4 * LOOP_TO, WORK + LAG):
                step(n // 4, n % 4)
            steps_before = steps[0]
            with v.If(fast == 1):
                attend(1)
            with v.Else():
                steps[0] = steps_before
                for b in range(B):
                    token_stats(b)
                for b in range(B):
                    scale_tokens(b)
                    add_projection(b)


NAMES = ["L0_attn_x", "L0_attn_Wq", "L0_attn_Wk", "L0_attn_Wv", "L0_attn_Wo", "L0_attn_W_down_kv",
         "L0_attn_W_up_k", "L0_attn_W_up_v", "L0_ffn_Wr", "L0_ffn_br", "L0_ffn_W1", "L0_ffn_b1",
         "L0_ffn_W2", "L0_ffn_b2", "L0_ffn_ln_w", "L0_ffn_ln_b"]


def kernel(**inputs):
    import numpy as np
    import concourse.bacc as bacc
    from concourse.bass_utils import run_bass_kernel_spmd

    nc = bacc.Bacc("TRN2", target_bir_lowering=False, num_devices=1)
    arrays = {name: np.ascontiguousarray(inputs[name]) for name in NAMES}
    at = np.arange(S, dtype=np.float32)
    arrays["decay"] = np.exp(np.float32(-0.01 * 0.01) * np.abs(at[:, None] - at[None, :])).astype(np.float32)
    rate = 0.01 * 0.01
    place = np.arange(S, dtype=np.float64)
    arrays["fold"] = np.ascontiguousarray(np.broadcast_to(
        np.stack([np.exp(-rate * place), np.exp(rate * place)]).astype(np.float32), (P, 2, S)))
    arrays["mend"] = np.exp(-2 * rate * np.maximum(place[S - P:, None] - place[None, :], 0)).astype(np.float32)
    arrays["head_ones"] = np.tile(np.eye(HEADS, dtype=np.float32), (HD, 1))
    arrays["below"] = np.triu(np.ones((P, P), np.float32), 1)
    arrays["counting"] = np.ascontiguousarray(np.broadcast_to(np.arange(WORK, dtype=np.float32), (P, WORK)))
    arrays["identity"] = np.eye(P, dtype=np.float32)
    arrays = {n: arrays[n] for n in NAMES + ["decay", "identity", "fold", "mend", "head_ones", "below", "counting"]}
    aps = [nc.dram_tensor(n, a.shape, mybir.dt.from_np(a.dtype), kind="ExternalInput").ap() for n, a in arrays.items()]
    out = nc.dram_tensor("out", (B, S, D), fp32, kind="ExternalOutput").ap()
    build(nc, *aps, out)
    result = run_bass_kernel_spmd(nc, [arrays], core_ids=[0])
    return result.results[0]["out"]
```
